# Optimizing a Trainium2 kernel written in Bass

```python
import numpy as np
import jax
import jax.numpy as jnp

def _softmax(x, axis=-1):
    return jax.nn.softmax(x, axis=axis)
def _gelu(x):
    return jax.nn.gelu(x, approximate=True)
def _silu(x):
    return jax.nn.silu(x)
def _sigmoid(x):
    return jax.nn.sigmoid(x)
def _layernorm(x, axis=-1, eps=1e-5):
    m = jnp.mean(x, axis=axis, keepdims=True)
    v = jnp.var(x, axis=axis, keepdims=True)
    return (x - m) / jnp.sqrt(v + eps)
def _scatter_add(tgt, idx, src, axis=0):
    return tgt.at[idx].add(src)
def _segment_sum(src, seg, n):
    return jax.ops.segment_sum(src, seg, n)

kernel_name = 'mk_adj_resnorm_d1_adj_256_d9412f'

def setup_inputs(seed: int = 0):
    np.random.seed(seed)
    _w = jnp.asarray
    def _rec_inputs():
        import jax
        import jax.numpy as jnp
        _gk = jax.random.key(seed)
        x = -0.0005207 + 1.001 * jax.random.normal(jax.random.fold_in(_gk, 1), (8, 2048, 256), jnp.float32)
        _w = (1.0 + jnp.arange(2048, dtype=jnp.float32)) ** -0.5
        _w = _w / _w.mean()
        _pij = jnp.clip(0.015625 * _w[:, None] * _w[None, :], 0.0, 1.0)
        _a = jax.random.uniform(jax.random.fold_in(_gk, 2), (8, 2048, 2048)) < _pij
        adj = _a.astype(jnp.int32)
        return x, adj
    x, adj = _rec_inputs()
    def _L0_gnn_setup():
        import jax, jax.numpy as jnp
        import numpy as np
        B, N, D = (8, 1024, 256)
        H, HO = (4, 64)
        T = 5
        NEG = -1000000000.0
        EPS = 1e-06
        key = jax.random.key(seed)
        ks = jax.random.split(key, 6)
        nodes_embed = jax.random.normal(ks[0], (B, N, D), dtype=jnp.float32)
        node_adj = jax.random.randint(ks[1], (B, N, N), 0, T + 1)
        W = jax.random.normal(ks[2], (H, D, HO), dtype=jnp.float32) * (1.0 / np.sqrt(D))
        a_src = jax.random.normal(ks[3], (H, T, HO), dtype=jnp.float32) * 0.1
        a_dst = jax.random.normal(ks[4], (H, T, HO), dtype=jnp.float32) * 0.1
        bias = jnp.zeros((H, HO), dtype=jnp.float32)
        ln_gamma = jnp.ones((H, HO), dtype=jnp.float32)
        ln_beta = jnp.zeros((H, HO), dtype=jnp.float32)
        return {'nodes_embed': nodes_embed, 'node_adj': node_adj, 'W': W, 'a_src': a_src, 'a_dst': a_dst, 'bias': bias, 'ln_gamma': ln_gamma, 'ln_beta': ln_beta}
    _L0_gnn_all = _L0_gnn_setup()
    _L0_gnn_in = {k: v for k, v in _L0_gnn_all.items() if k in ('W', 'a_src', 'a_dst', 'bias', 'ln_gamma', 'ln_beta', )}
    del _L0_gnn_all

    return {
        "x": x,
        "adj": adj,
        "L0_gnn_W": _L0_gnn_in["W"],
        "L0_gnn_a_src": _L0_gnn_in["a_src"],
        "L0_gnn_a_dst": _L0_gnn_in["a_dst"],
        "L0_gnn_bias": _L0_gnn_in["bias"],
        "L0_gnn_ln_gamma": _L0_gnn_in["ln_gamma"],
        "L0_gnn_ln_beta": _L0_gnn_in["ln_beta"],
    }

def reference(x, adj, L0_gnn_W, L0_gnn_a_src, L0_gnn_a_dst, L0_gnn_bias, L0_gnn_ln_gamma, L0_gnn_ln_beta):
    import jax
    import jax.numpy as jnp
    def _L0_gnn_ref(nodes_embed, node_adj, W, a_src, a_dst, bias, ln_gamma, ln_beta):
        import jax, jax.numpy as jnp
        import numpy as np
        B, N, D = (8, 1024, 256)
        H, HO = (4, 64)
        T = 5
        NEG = -1000000000.0
        EPS = 1e-06
        h = jnp.einsum('bnd,hde->bhne', nodes_embed, W)
        e_src = jnp.einsum('bhne,hte->bhtn', h, a_src)
        e_dst = jnp.einsum('bhne,hte->bhtn', h, a_dst)
        n_types = a_src.shape[1]
        weight = jnp.zeros(h.shape[:2] + (h.shape[2], h.shape[2]), dtype=h.dtype)
        for t in range(n_types):
            mask = (node_adj == t + 1).astype(h.dtype)[:, None]
            weight = weight + mask * (e_src[:, :, t, :, None] + e_dst[:, :, t, None, :])
        weight = jax.nn.leaky_relu(weight, negative_slope=0.01)
        weight = jnp.where(node_adj[:, None] == 0, NEG, weight)
        attention = jax.nn.softmax(weight, axis=-1)
        dst = jnp.einsum('bhij,bhje->bhie', attention, h) + bias[None, :, None, :]
        out = jax.nn.relu(dst) + h
        mu = out.mean(axis=-1, keepdims=True)
        var = out.var(axis=-1, keepdims=True)
        out = (out - mu) / jnp.sqrt(var + EPS) * ln_gamma[None, :, None, :] + ln_beta[None, :, None, :]
        b, hh, n, e = out.shape
        return out.transpose(0, 2, 1, 3).reshape(b, n, hh * e)

    x = _layernorm(x + _L0_gnn_ref(x, adj, L0_gnn_W, L0_gnn_a_src, L0_gnn_a_dst, L0_gnn_bias, L0_gnn_ln_gamma, L0_gnn_ln_beta), axis=-1)
    return x


_drawn_inputs = setup_inputs


def setup_inputs(seed=0):
    import zlib

    import numpy as np

    out = dict(_drawn_inputs(seed))
    spreads = {'L0_gnn_bias': (0.0, 0.1), 'L0_gnn_ln_gamma': (1.0, 0.2), 'L0_gnn_ln_beta': (0.0, 0.1)}
    factors = {}
    for name, (base, spread) in spreads.items():
        noise = np.random.default_rng([zlib.crc32(name.encode()), seed]).standard_normal(out[name].shape)
        drawn = base * np.exp(spread * noise) if base else spread * noise
        out[name] = jnp.asarray(drawn.astype(out[name].dtype))
    for name, factor in factors.items():
        out[name] = (out[name] * factor).astype(out[name].dtype)
    return out
```

```python
import concourse.bass as bass
from concourse import mybir
from contextlib import ExitStack

FP32 = mybir.dt.float32
BF16 = mybir.dt.bfloat16
I32 = mybir.dt.int32
FP16 = mybir.dt.float16
ALU = mybir.AluOpType
ACT = mybir.ActivationFunctionType
AX = mybir.AxisListType


def gat_layer(nc, x, adj, W, a_src, a_dst, bias, gamma, beta, out):
    B, N, D = x.shape
    H, _, HO = W.shape
    T = a_src.shape[1]
    P = 128
    NT = N // P
    GI = 8
    NG = NT // GI
    IW = GI * P
    HP = 2
    NP = H // HP
    CJ = 2
    NCB = 4
    NCG = NT // CJ
    DC = D // P
    HD = H * HO
    EC = 2 * H
    PW = HD + EC
    AW = HO + 1
    PERBANK = 512 // (2 * AW)
    NPAIR = GI * HP
    NAB = -(-NPAIR // PERBANK)
    LN1_EPS, LN2_EPS = 1e-6, 1e-5
    SLOPE = 0.01
    BIG = 1e30
    SCALE = 4096.0
    UPG = NP * NT

    ctx = ExitStack()
    with ctx:
        def sb(name, shape, dt=FP32):
            return ctx.enter_context(nc.sbuf_tensor(name, shape, dt))

        def pb(name, shape, dt=FP32):
            return ctx.enter_context(nc.psum_tensor(name, shape, dt))

        def sem(name):
            return ctx.enter_context(nc.semaphore(name))

        score_rows = nc.dram_tensor("score_rows", (2, H * NT, P), FP32, kind="Internal").ap()

        ident_b = sb("ident_b", [P, P], BF16)
        ident_f = sb("ident_f", [P, P])
        zeros = sb("zeros", [P, PERBANK * 2 * AW], BF16)
        w_cat = sb("w_cat", [P, DC, PW])
        bias_b = sb("bias_b", [P, HD])
        gamma_b = sb("gamma_b", [P, HD])
        beta_b = sb("beta_b", [P, HD])
        minus_half = sb("minus_half", [P, GI * H])
        adj_b = sb("adj_b", [P, NCB, GI, CJ * P], BF16)
        mask = sb("mask", [P, NT, IW], BF16)
        s_bc = sb("s_bc", [P, NP, HP, IW])
        he = sb("he", [P, NT + NT // 2, PW])
        rh = sb("rh", [P, NT, H, 2, 2 * AW], FP16)
        rf = sb("rf", [P, NT, H, 2, AW], FP16)
        v = sb("v", [P, NT, AW])
        d_big = sb("d_big", [P, 2, NT * H])
        fac = sb("fac", [P, 2, NT, H])
        g_fac = sb("g_fac", [P, 2, NT, H])
        r = sb("r", [P, 2, HP, IW], BF16)
        b_pos = sb("b_pos", [P, 2, HP, IW], BF16)
        x_pair = sb("x_pair", [P, 2, D])
        xT = sb("xT", [P, 2, DC, P])
        o = sb("o", [P, NPAIR, 2 * AW])
        y = sb("y", [P, NG, GI, HD])
        xr = sb("xr", [P, GI, HD])
        seen = sb("seen", [P, GI * CJ * P // 4], I32)
        wait_pad = sb("wait_pad", [P, 1])
        rden = sb("rden", [P, NPAIR])
        dmin = sb("dmin", [P, 2])
        mean1 = sb("mean1", [P, GI, H])
        var1 = sb("var1", [P, GI * H])
        rstd1 = sb("rstd1", [P, GI * H])
        mean2 = sb("mean2", [P, NG, GI])
        var2 = sb("var2", [P, GI])
        var2e = sb("var2e", [P, GI])
        rstd2 = sb("rstd2", [P, GI])
        nmr2 = sb("nmr2", [P, GI])
        dmax_l = sb("dmax_l", [P, H])
        dmax = sb("dmax", [P, H])
        d_sh = sb("d_sh", [P, NT, H])
        sg_sh = sb("sg_sh", [P, NT, H])
        s_hn = sb("s_hn", [P, 2, H * NT])
        sT = sb("sT", [P, P])
        eabs = sb("eabs", [P, 2])
        a_rows = y[0:2 * H, 0, 0, 0:HO]
        aT = y[0:HO, 0, 1, 0:EC]
        wT = y[0:HO, 1, :, 0:P]

        acc = [pb(f"acc{i}", [P, 512]) for i in range(NAB)]
        mT = pb("mT", [P, IW], BF16)
        pj = pb("pj", [P, 512])

        def acc_of(it, k, part=None):
            n = it * HP + k
            c = (n % PERBANK) * 2 * AW
            lo, hi = {None: (0, 2 * AW), "E": (0, AW), "F": (AW, 2 * AW)}[part]
            return acc[n // PERBANK][:, c + lo:c + hi]

        def bank_pairs(k):
            return PERBANK * k, min(PERBANK * (k + 1), NPAIR)

        ACT_BANKS = range(0, 4)
        DVE_BANKS = range(4, NAB)

        s_id = sem("s_id")
        s_const = sem("s_const")
        s_w = sem("s_w")
        s_vec = sem("s_vec")
        s_setup_pe = sem("s_setup_pe")
        s_setup_act = sem("s_setup_act")
        s_memset = sem("s_memset")
        adj_loaded = [sem(f"adj_loaded{c}") for c in range(NCB)]
        adj_checked = sem("adj_checked")
        mask_ready = sem("mask_ready")
        mask_copied = sem("mask_copied")
        r_ready = sem("r_ready")
        b_ready = sem("b_ready")
        pv_done = sem("pv_done")
        acc_out_act = sem("acc_out_act")
        acc_out_dve = sem("acc_out_dve")
        xp_loaded = sem("xp_loaded")
        tx_done = sem("tx_done")
        xt_copied = sem("xt_copied")
        mm_done = sem("mm_done")
        he_copied = sem("he_copied")
        stats_done = sem("stats_done")
        dmax_done = sem("dmax_done")
        pro_done = sem("pro_done")
        exps_done = sem("exps_done")
        fac_done = sem("fac_done")
        v_done = sem("v_done")
        hi_done = sem("hi_done")
        lo_done = sem("lo_done")
        neg_done = sem("neg_done")
        st_vec = sem("st_vec")
        st_pe = sem("st_pe")
        st_act = sem("st_act")
        rows_stored = sem("rows_stored")
        s_loaded = [sem(f"s_loaded{p}") for p in range(NP)]
        y_chain = sem("y_chain")
        centred = sem("centred")
        squared1 = sem("squared1")
        var1_done = sem("var1_done")
        norm1 = sem("norm1")
        xr_loaded = sem("xr_loaded")
        sum2_done = sem("sum2_done")
        squared2 = sem("squared2")
        var2_done = sem("var2_done")
        norm2 = sem("norm2")
        pool_chain1 = sem("pool_chain1")
        pool_chain2 = sem("pool_chain2")
        stored = [sem(f"stored{g}") for g in range(NG)]

        YK = 9
        SK = 2
        NITEM = 2 * HP
        HALF = NT // 2

        block = ctx.enter_context(nc.Block())

        def known(*counts):
            return all(isinstance(n, int) for n in counts)

        def batches(eng, body):
            body(0, True, B == 1)
            if B > 2:
                with eng.Fori(1, B - 1) as b:
                    body(b, False, False)
            if B > 1:
                body(B - 1, False, True)

        def he_rows(b, t, n=1):
            if isinstance(t, int) and t < HALF:
                return bass.ds(t, n)
            return bass.ds(HALF + (b % 2) * HALF + (t - HALF), n)

        halves = ((0, HALF), (HALF, HALF))

        @block.sync
        def _(sp):
            for c in range(DC):
                sp.dma_start(w_cat[:, c, 0:HD].rearrange("p (h e) -> p h e", h=H),
                             W[:, c * P:(c + 1) * P, :].rearrange("h p e -> p h e")).then_inc(s_w, 16)
            sp.dma_start(a_rows[0:H, :], a_src[:, 0, :]).then_inc(s_w, 16)
            sp.dma_start(a_rows[H:EC, :], a_dst[:, 0, :]).then_inc(s_w, 16)
            for dst, src in ((bias_b, bias), (gamma_b, gamma), (beta_b, beta)):
                sp.dma_start(dst[:, :], src.rearrange("(o h) e -> o (h e)", o=1).to_broadcast((P, HD)))\
                  .then_inc(s_vec, 16)

            def load_pair(b, q):
                k = b * HALF + q
                if not (known(k) and k == 0):
                    sp.wait_ge(tx_done, k)
                sp.dma_start(x_pair[:, :, :],
                             x[b, bass.ds(q * 2 * P, 2 * P), :].rearrange("(t p) d -> p t d", p=P))\
                  .then_inc(xp_loaded, 16)

            def load_scores(b, g, p):
                gg = b * NG + g
                if not (known(gg) and gg == 0):
                    sp.wait_ge(r_ready, HP * ((gg - 1) * UPG + (p + 1) * NT))
                sp.dma_start(s_bc[:, p, :, :],
                             score_rows[b % 2, :, :].rearrange("(o h t) n -> o h (t n)", o=1, h=H)
                             [:, p * HP:(p + 1) * HP, g * IW:(g + 1) * IW].to_broadcast((P, HP, IW)))\
                  .then_inc(s_loaded[p], 16)

            def store_rows(b):
                sp.wait_ge(st_act, b + 1)
                sp.dma_start(score_rows[b % 2, :, :], sT[0:H * NT, :]).then_inc(rows_stored, 16)
                sp.wait_ge(rows_stored, (b + 1) * 16)

            def load_xr(gg, b, g):
                if not (known(gg) and gg == 0):
                    sp.wait_ge(norm1, gg)
                sp.dma_start(xr[:, :, :], x[b, g * IW:(g + 1) * IW, :].rearrange("(t p) d -> p t d", p=P))\
                  .then_inc(xr_loaded, 16)

            def store_out(gg, b, g):
                sp.wait_ge(norm2, gg + 1)
                sp.dma_start(out[b, g * IW:(g + 1) * IW, :].rearrange("(t p) d -> p t d", p=P),
                             y[:, g, :, :]).then_inc(stored[g], 16)

            sp.wait_ge(s_setup_act, 2)
            load_pair(0, 0)
            with sp.Fori(1, HALF) as q:
                load_pair(0, q)
            store_rows(0)
            load_scores(0, 0, 0)
            load_scores(0, 0, 1)

            def body(b, first, last):
                gg = b * NG
                if not first:
                    load_xr(gg - 1, b - 1, 1)
                if not first:
                    store_out(gg - 2, b - 1, 0)
                load_scores(b, 1, 0)
                load_scores(b, 1, 1)
                load_xr(gg, b, 0)
                for q in range(HALF):
                    if not last:
                        load_pair(b + 1, q)
                    if q == 5 and not first:
                        store_out(gg - 1, b - 1, 1)
                if not last:
                    store_rows(b + 1)
                    load_scores(b + 1, 0, 0)
                    load_scores(b + 1, 0, 1)

            batches(sp, body)
            load_xr(B * NG - 1, B - 1, 1)
            store_out(B * NG - 2, B - 1, 0)
            store_out(B * NG - 1, B - 1, 1)
            for g in range(NG):
                sp.wait_ge(stored[g], 16 * B)

        @block.gpsimd
        def _(pool):
            nc.gpsimd.memset(ident_b[:, :], 0.0)
            nc.gpsimd.memset(ident_f[:, :], 0.0)
            nc.gpsimd.memset(minus_half[:, :], -0.5)
            nc.gpsimd.memset(zeros[:, :], 0.0)
            nc.gpsimd.memset(seen[:, :], 0).then_inc(s_id, 1)
            pool.wait_ge(s_id, 1)
            for m in (ident_b, ident_f):
                last_ins = nc.gpsimd.affine_select(out=m[:, :], in_=m[:, :], compare_op=ALU.not_equal,
                                                   fill=1.0, base=0, pattern=[[-1, P]],
                                                   channel_multiplier=1)
            last_ins.then_inc(s_const, 1)
            pool.wait_ge(s_const, 1)

            def load_adj(b, g, c):
                gg = b * NG + g
                if not (known(gg) and gg == 0 and c < NCB):
                    n = gg * NCG + c - NCB
                    pool.wait_ge(adj_checked, 2 * (n + 1))
                    pool.wait_ge(mask_ready, (n + 1) * CJ)
                j0 = c * CJ * P
                nc.gpsimd.dma_start(
                    adj_b[:, c % NCB, :, :],
                    adj[b, g * IW:(g + 1) * IW, j0:j0 + CJ * P].rearrange("(t p) j -> p t j", p=P))\
                    .then_inc(adj_loaded[c % NCB], 16)

            def next_group(b, g, last):
                if g + 1 < NG:
                    for c in range(NCB):
                        load_adj(b, g + 1, c)
                elif not last:
                    for c in range(NCB):
                        load_adj(b + 1, 0, c)

            for c in range(NCB):
                load_adj(0, 0, c)

            def max_of_all(b):
                pool.wait_ge(stats_done, SK * b + 1)
                nc.gpsimd.tensor_tensor(wait_pad[:, :], minus_half[:, 0:1], minus_half[:, 0:1], ALU.mult)
                nc.gpsimd.partition_all_reduce(dmax[:, :], dmax_l[:, :], P, bass.bass_isa.ReduceOp.max)\
                    .then_inc(dmax_done, 1)

            def weights(b, p, m):
                h, f = p * HP + m // 2, m % 2
                n = (b * NP + p) * NITEM + m
                pool.wait_ge(fac_done, b + 1)
                if not (known(n) and n == 0):
                    pool.wait_ge(lo_done, n)
                for t, w in halves:
                    nc.gpsimd.tensor_tensor(
                        v[:, t:t + w, 0:HO], he[:, he_rows(b, t, w), h * HO:(h + 1) * HO],
                        fac[:, f, t:t + w, h:h + 1].to_broadcast((P, w, HO)), ALU.mult)
                nc.gpsimd.tensor_copy(v[:, :, HO:AW], fac[:, f, :, h:h + 1]).then_inc(v_done, 1)
                pool.wait_ge(hi_done, n + 1)
                part = (rh[:, :, h, :, 0:AW], rf[:, :, h, :, :])[f]
                nc.gpsimd.tensor_tensor(part[:, :, 1, :], v[:, :, :], part[:, :, 0, :], ALU.subtract)\
                    .then_inc(lo_done, 1)

            def centre(gg, g):
                pool.wait_ge(y_chain, YK * NP * (gg + 1))
                yv = y[:, g, :, :].rearrange("p t (h e) -> p (t h) e", h=H)
                nc.gpsimd.tensor_tensor(
                    yv, yv, mean1[:, :, :].rearrange("p t h -> p (t h)").unsqueeze(2).to_broadcast((P, GI * H, HO)),
                    ALU.subtract).then_inc(centred, 1)

            def normalise1(gg, g):
                n = 4 * gg
                pool.wait_ge(var1_done, 2 * gg + 2)
                nc.gpsimd.tensor_tensor(rstd1[:, :], var1[:, :], minus_half[:, :], ALU.pow).then_inc(pool_chain1, 1)
                pool.wait_ge(pool_chain1, n + 1)
                yh = y[:, g, :, :].rearrange("p t (h e) -> p (t h) e", h=H)
                nc.gpsimd.tensor_tensor(yh, yh, rstd1[:, :].unsqueeze(2).to_broadcast((P, GI * H, HO)),
                                        ALU.mult).then_inc(pool_chain1, 1)
                pool.wait_ge(pool_chain1, n + 2)
                yt = y[:, g, :, :]
                nc.gpsimd.tensor_tensor(yt, yt, gamma_b[:, :].unsqueeze(1).to_broadcast((P, GI, HD)),
                                        ALU.mult).then_inc(pool_chain1, 1)
                pool.wait_ge(pool_chain1, n + 3)
                nc.gpsimd.tensor_tensor(yt, yt, beta_b[:, :].unsqueeze(1).to_broadcast((P, GI, HD)),
                                        ALU.add).then_inc(pool_chain1, 1)
                pool.wait_ge(pool_chain1, n + 4)
                pool.wait_ge(xr_loaded, 16 * (gg + 1))
                nc.gpsimd.tensor_tensor(yt, yt, xr[:, :, :], ALU.add).then_inc(norm1, 1)

            def normalise2(gg, g):
                n = 3 * gg
                pool.wait_ge(var2_done, gg + 1)
                nc.gpsimd.tensor_tensor(rstd2[:, :], var2e[:, :], minus_half[:, 0:GI], ALU.pow)\
                    .then_inc(pool_chain2, 1)
                pool.wait_ge(pool_chain2, n + 1)
                nc.gpsimd.tensor_tensor(nmr2[:, :], mean2[:, g, :], rstd2[:, :], ALU.mult)\
                    .then_inc(pool_chain2, 1)
                pool.wait_ge(pool_chain2, n + 2)
                yt = y[:, g, :, :]
                nc.gpsimd.tensor_tensor(yt, yt, rstd2[:, :].unsqueeze(2).to_broadcast((P, GI, HD)), ALU.mult)\
                    .then_inc(pool_chain2, 1)
                pool.wait_ge(pool_chain2, n + 3)
                nc.gpsimd.tensor_tensor(yt, yt, nmr2[:, :].unsqueeze(2).to_broadcast((P, GI, HD)), ALU.add)\
                    .then_inc(norm2, 1)

            max_of_all(0)
            for m in range(NITEM):
                weights(0, 0, m)

            def body(b, first, last):
                for g in range(NG):
                    gg = b * NG + g
                    if not (first and g == 0):
                        centre(gg - 1, 1 - g)
                    for c in range(NCB, NCG):
                        if g == 0:
                            weights(b, 1, c - NCB)
                        load_adj(b, g, c)
                        if c == NCB + 1 and not first:
                            normalise2(gg - 2, g)
                    next_group(b, g, last)
                    if not (first and g == 0):
                        normalise1(gg - 1, 1 - g)
                    if g == NG - 1 and not last:
                        max_of_all(b + 1)
                        for m in range(NITEM):
                            weights(b + 1, 0, m)

            batches(pool, body)
            G = B * NG
            centre(G - 1, 1)
            normalise2(G - 2, 0)
            normalise1(G - 1, 1)
            normalise2(G - 1, 1)

        @block.scalar
        def _(act):
            act.wait_ge(s_setup_pe, 1)
            nc.scalar.activation(aT, pj[0:HO, 0:EC], ACT.Copy)
            nc.scalar.activation(wT[:, 0:4, :], acc[0][0:HO, :].rearrange("p (k n) -> p k n", n=P), ACT.Copy)
            nc.scalar.activation(wT[:, 4:8, :], acc[1][0:HO, :].rearrange("p (k n) -> p k n", n=P), ACT.Copy)\
                .then_inc(s_setup_act, 1)
            act.wait_ge(s_setup_pe, 2)
            nc.scalar.activation(w_cat[:, :, HD:PW].rearrange("p c (k h) -> p c k h", k=2),
                                 acc[2][:, 0:DC * EC].rearrange("p (c h k) -> p c k h", c=DC, k=2), ACT.Copy)\
                .then_inc(s_setup_act, 1)

            def copy_xT(b, q):
                k = b * HALF + q
                act.wait_ge(tx_done, k + 1)
                if not (known(k) and k == 0):
                    act.wait_ge(mm_done, 2 * k)
                nc.scalar.activation(xT[:, :, :, :], pj[:, :].rearrange("p (a c n) -> p a c n", a=2, c=DC),
                                     ACT.Copy).then_inc(xt_copied, 1)

            def copy_he(b, q, i, slots):
                k = b * HALF + q
                act.wait_ge(mm_done, 2 * k + i + 1)
                nc.scalar.activation(he[:, slots, :], pj[:, 0:PW].unsqueeze(1), ACT.Copy)\
                    .then_inc(he_copied, 1)

            def factors(b):
                act.wait_ge(pro_done, b + 1)
                nc.scalar.activation(fac[:, 0, :, :], d_sh[:, :, :], ACT.Exp)
                nc.scalar.activation(fac[:, 1, :, :], d_sh[:, :, :], ACT.Exp, scale=SLOPE)
                nc.scalar.activation(g_fac[:, bass.ds(b % 2, 1), :, :].rearrange("p o t h -> p (o t) h"),
                                     sg_sh[:, :, :], ACT.Exp, scale=SLOPE - 1.0).then_inc(exps_done, 1)

            def rows(b):
                act.wait_ge(st_pe, b + 1)
                if not (known(b) and b == 0):
                    act.wait_ge(rows_stored, 16 * b)
                nc.scalar.activation(sT[:, :], pj[:, 0:P], ACT.Copy).then_inc(st_act, 1)

            def high_part(b, p, m):
                n = (b * NP + p) * NITEM + m
                h, f = p * HP + m // 2, m % 2
                act.wait_ge(v_done, n + 1)
                if m == 0 and not (known(b) and b == 0):
                    act.wait_ge(pv_done, (b * NG - 1) * UPG + (p + 1) * NT)
                part = (rh[:, :, h, :, 0:AW], rf[:, :, h, :, :])[f]
                nc.scalar.activation(part[:, :, 0, :], v[:, :, :], ACT.Copy).then_inc(hi_done, 1)

            def positive(b, g, p, u, k):
                uu = (b * NG + g) * UPG + p * NT + u
                if u == 0 and k == 0:
                    act.wait_ge(s_loaded[p], 16 * (b * NG + g + 1))
                    act.wait_ge(pro_done, b + 1)
                if k == 0 and not (known(uu) and uu < 2):
                    act.wait_ge(b_ready, uu - 1)
                col = u * H + p * HP + k
                bias_ap = d_big[:, bass.ds(b % 2, 1), col:col + 1].rearrange("p o c -> p (o c)")
                nc.scalar.activation(r[:, u % 2, k, :], s_bc[:, p, k, :], ACT.Relu, bias=bias_ap, scale=BIG)\
                    .then_inc(r_ready, 1)

            def square1(gg, g):
                act.wait_ge(centred, gg + 1)
                if not (known(gg) and gg == 0):
                    act.wait_ge(squared2, gg)
                nc.scalar.activation(o_flat.rearrange("p (t e) -> p t e", e=HO),
                                     y[:, g, :, :].rearrange("p t (h e) -> p (t h) e", h=H),
                                     ACT.Square).then_inc(squared1, 1)

            o_flat = o[:, :, :].rearrange("p n w -> p (n w)")[:, 0:GI * HD]

            def square2(gg, g):
                act.wait_ge(sum2_done, 2 * gg + 2)
                if not (known(gg) and gg == 0):
                    act.wait_ge(var2_done, gg)
                for it in range(GI):
                    ins = nc.scalar.activation(o_flat[:, it * HD:(it + 1) * HD], y[:, g, it, :], ACT.Square,
                                               bias=mean2[:, g, it:it + 1], accum_out=var2[:, it:it + 1])
                ins.then_inc(squared2, 1)

            def acc_out(b, g, p):
                pp = (b * NG + g) * NP + p
                act.wait_ge(pv_done, (pp + 1) * NT)
                if p == 0:
                    if not (known(pp) and pp == 0):
                        act.wait_ge(var1_done, 2 * (b * NG + g))
                        act.wait_ge(y_chain, YK * pp)
                else:
                    act.wait_ge(y_chain, YK * pp)
                for k in ACT_BANKS:
                    a, e = bank_pairs(k)
                    ins = nc.scalar.activation(o[:, a:e, :].rearrange("p n w -> p (n w)"),
                                               acc[k][:, 0:(e - a) * 2 * AW], ACT.Copy)
                ins.then_inc(acc_out_act, 1)

            for q in range(HALF):
                copy_xT(0, q)
                for i in range(2):
                    copy_he(0, q, i, he_rows(0, 2 * q + i))
            factors(0)
            rows(0)
            for m in range(NITEM):
                high_part(0, 0, m)

            def body(b, first, last):
                for g in range(NG):
                    gg = b * NG + g
                    for p in range(NP):
                        for u in range(NT):
                            for k in range(HP):
                                positive(b, g, p, u, k)
                                if g == 1 and p == 0 and not last:
                                    q, step = u // 2, (u % 2) * 2 + k
                                    if step == 1:
                                        copy_xT(b + 1, q)
                                    if step == 2:
                                        copy_he(b + 1, q, 0, he_rows(b + 1, 2 * q))
                                    if step == 3:
                                        copy_he(b + 1, q, 1, he_rows(b + 1, 2 * q + 1))
                            if p == 0 and u == 6 and not (first and g == 0):
                                square1(gg - 1, 1 - g)
                            if p == 1 and u == 13 and not (first and g == 0):
                                square2(gg - 1, 1 - g)
                            if g == 0 and p == 0 and u in (2, 5, 7, 9):
                                high_part(b, 1, (2, 5, 7, 9).index(u))
                            if g == 1 and p == 1 and not last:
                                if u == 1:
                                    factors(b + 1)
                                    rows(b + 1)
                                if u in (9, 11, 14, 15):
                                    high_part(b + 1, 0, (9, 11, 14, 15).index(u))
                        acc_out(b, g, p)

            batches(act, body)
            G = B * NG
            square1(G - 1, 1)
            square2(G - 1, 1)

        @block.vector
        def _(dve):
            nc.vector.memset(eabs[:, :], 0.0)
            nc.vector.memset(dmin[:, :], 1.0).then_inc(s_memset, 1)

            def stats(b):
                dve.wait_ge(he_copied, NT * (b + 1))
                if not (known(b) and b == 0):
                    dve.wait_ge(dmax_done, b)
                    dve.wait_ge(st_pe, b)
                for t, m in halves:
                    rows_ = he[:, he_rows(b, t, m), :]
                    nc.vector.tensor_copy(s_hn[:, 0, :].rearrange("p (h t) -> p t h", h=H)[:, t:t + m, :],
                                          rows_[:, :, HD:HD + H])
                    ins = nc.vector.tensor_copy(s_hn[:, 1, :].rearrange("p (h t) -> p t h", h=H)[:, t:t + m, :],
                                                rows_[:, :, HD + H:PW])
                ins.then_inc(st_vec, 1)
                dve.wait_ge(st_vec, b + 1)
                nc.vector.tensor_reduce(dmax_l[:, :], s_hn[:, 1, :].rearrange("p (h t) -> p h t", h=H), AX.X, ALU.max)\
                    .then_inc(stats_done, 1)
                nc.vector.tensor_reduce(eabs[:, 1:2], s_hn[:, :, :].rearrange("p k n -> p (k n)"), AX.X, ALU.max,
                                        apply_absolute_value=True).then_inc(stats_done, 1)

            def shifts(b):
                dve.wait_ge(stats_done, SK * b + 2)
                nc.vector.tensor_tensor(eabs[:, 0:1], eabs[:, 0:1], eabs[:, 1:2], ALU.max)
                nc.vector.tensor_scalar(d_big[:, bass.ds(b % 2, 1), :].rearrange("p o (t h) -> p (o h) t", h=H),
                                        s_hn[:, 1, :].rearrange("p (h t) -> p h t", h=H), BIG, None, ALU.mult)
                dve.wait_ge(dmax_done, b + 1)
                if not (known(b) and b == 0):
                    dve.wait_ge(exps_done, b)
                gmax = dmax[:, :].unsqueeze(1).to_broadcast((P, NT, H))
                nc.vector.tensor_tensor(sg_sh[:, :, :], s_hn[:, 0, :].rearrange("p (h t) -> p t h", h=H), gmax, ALU.add)
                nc.vector.tensor_tensor(d_sh[:, :, :], s_hn[:, 1, :].rearrange("p (h t) -> p t h", h=H), gmax,
                                        ALU.subtract).then_inc(pro_done, 1)

            def scale_factors(b):
                dve.wait_ge(exps_done, b + 1)
                ff = fac[:, :, :, :].rearrange("p f t h -> p (f t h)")
                nc.vector.tensor_scalar(ff, ff, SCALE, None, ALU.mult).then_inc(fac_done, 1)

            def negate(b, p):
                dve.wait_ge(lo_done, (b * NP + p + 1) * NITEM)
                for k in range(HP):
                    h = p * HP + k
                    for part in range(2):
                        ins = nc.vector.tensor_scalar(rh[:, :, h, part, AW:2 * AW], rf[:, :, h, part, :], -1.0, None,
                                                      ALU.mult)
                ins.then_inc(neg_done, 1)

            def copy_mask(b, g, u):
                jj = (b * NG + g) * NT + u
                dve.wait_ge(mask_ready, jj + 1)
                if not (known(b, g) and b == 0 and g == 0):
                    dve.wait_ge(pv_done, (b * NG + g - 1) * UPG + NT + u + 1)
                nc.vector.tensor_copy(mask[:, u, :], mT[:, :]).then_inc(mask_copied, 1)

            def probs(b, g, p, u):
                uu = (b * NG + g) * UPG + p * NT + u
                if p == 0:
                    dve.wait_ge(mask_copied, (b * NG + g) * NT + u + 1)
                dve.wait_ge(r_ready, HP * (uu + 1))
                if not (known(uu) and uu < 2):
                    dve.wait_ge(pv_done, uu - 1)
                nc.vector.tensor_tensor(b_pos[:, u % 2, :, :], r[:, u % 2, :, :],
                                        mask[:, u, :].unsqueeze(1).to_broadcast((P, HP, IW)), ALU.min)\
                    .then_inc(b_ready, 1)

            def check_adj(b, g, c):
                n = (b * NG + g) * NCG + c
                dve.wait_ge(adj_loaded[c % NCB], 16 * ((b * NG + g) * (NCG // NCB) + c // NCB + 1))
                bits = adj_b[:, c % NCB, :, :].rearrange("p t j -> p (t j)").bitcast(I32)
                w = GI * CJ * P // 4
                for i in range(2):
                    if not (known(n) and n == 0 and i == 0):
                        dve.wait_ge(adj_checked, 2 * n + i)
                    nc.vector.tensor_tensor(seen[:, :], seen[:, :], bits[:, i * w:(i + 1) * w],
                                            ALU.bitwise_or).then_inc(adj_checked, 1)

            def finish_rows(b, g, p):
                pp = (b * NG + g) * NP + p
                gg = b * NG + g
                n = YK * pp
                dve.wait_ge(pv_done, (pp + 1) * NT)
                if p == 0 and not (known(pp) and pp == 0):
                    dve.wait_ge(var1_done, 2 * gg)
                for k in DVE_BANKS:
                    a, e = bank_pairs(k)
                    ins = nc.vector.tensor_copy(o[:, a:e, :].rearrange("p n w -> p (n w)"),
                                                acc[k][:, 0:(e - a) * 2 * AW])
                ins.then_inc(acc_out_dve, 1)
                dve.wait_ge(acc_out_dve, pp + 1)
                dve.wait_ge(acc_out_act, pp + 1)
                for it in range(GI):
                    gsc = g_fac[:, bass.ds(b % 2, 1), g * GI + it, p * HP:(p + 1) * HP]\
                        .rearrange("p o h -> p (o h)").unsqueeze(2).to_broadcast((P, HP, AW))
                    fs = o[:, it * HP:(it + 1) * HP, AW:2 * AW]
                    ins = nc.vector.tensor_tensor(fs, fs, gsc, ALU.mult)
                ins.then_inc(y_chain, 1)
                dve.wait_ge(y_chain, n + 1)
                nc.vector.tensor_tensor(o[:, :, 0:AW], o[:, :, 0:AW], o[:, :, AW:2 * AW], ALU.add)\
                    .then_inc(y_chain, 1)
                dve.wait_ge(y_chain, n + 2)
                den = o[:, :, HO:AW].rearrange("p n o -> p (n o)")
                nc.vector.tensor_reduce(dmin[:, 1:2], den, AX.X, ALU.min).then_inc(y_chain, 1)
                nc.vector.reciprocal(rden[:, :], den).then_inc(y_chain, 1)
                dve.wait_ge(y_chain, n + 4)
                nc.vector.tensor_tensor(dmin[:, 0:1], dmin[:, 0:1], dmin[:, 1:2], ALU.min)
                if p == 0 and not (known(gg) and gg < NG):
                    dve.wait_ge(stored[g], 16 * b)
                cols = slice(p * HP * HO, (p + 1) * HP * HO)
                yt = y[:, g, :, cols]
                yh = yt.rearrange("p t (h e) -> p t h e", h=HP)
                nc.vector.tensor_tensor(yh, o[:, :, 0:HO].rearrange("p (t h) e -> p t h e", h=HP),
                                        rden[:, :].rearrange("p (t h) -> p t h", h=HP).unsqueeze(3)
                                        .to_broadcast((P, GI, HP, HO)), ALU.mult).then_inc(y_chain, 1)
                dve.wait_ge(y_chain, n + 5)
                nc.vector.tensor_tensor(yt, yt, bias_b[:, cols].unsqueeze(1).to_broadcast((P, GI, HP * HO)),
                                        ALU.add).then_inc(y_chain, 1)
                dve.wait_ge(y_chain, n + 6)
                nc.vector.scalar_tensor_tensor(yt, yt, 0.0, he[:, he_rows(b, g * GI, GI), cols],
                                               ALU.max, ALU.add).then_inc(y_chain, 1)
                dve.wait_ge(y_chain, n + 7)
                if p == 0 and not (known(gg) and gg == 0):
                    dve.wait_ge(centred, gg)
                m1 = mean1[:, :, p * HP:(p + 1) * HP]
                nc.vector.tensor_reduce(m1, yh, AX.X, ALU.add).then_inc(y_chain, 1)
                dve.wait_ge(y_chain, n + 8)
                nc.vector.tensor_scalar(m1, m1, 1.0 / HO, None, ALU.mult).then_inc(y_chain, 1)

            def variance1(gg):
                dve.wait_ge(squared1, gg + 1)
                if not (known(gg) and gg == 0):
                    dve.wait_ge(norm1, gg)
                nc.vector.tensor_reduce(var1[:, :], o[:, :, :].rearrange("p n w -> p (n w)")[:, 0:GI * HD]
                                        .rearrange("p (t e) -> p t e", e=HO), AX.X, ALU.add).then_inc(var1_done, 1)
                dve.wait_ge(var1_done, 2 * gg + 1)
                nc.vector.tensor_scalar(var1[:, :], var1[:, :], 1.0 / HO, LN1_EPS, ALU.mult, ALU.add)\
                    .then_inc(var1_done, 1)

            def sum2(gg, g):
                dve.wait_ge(norm1, gg + 1)
                nc.vector.tensor_reduce(mean2[:, g, :], y[:, g, :, :], AX.X, ALU.add).then_inc(sum2_done, 1)
                dve.wait_ge(sum2_done, 2 * gg + 1)
                nc.vector.tensor_scalar(mean2[:, g, :], mean2[:, g, :], -1.0 / HD, None, ALU.mult)\
                    .then_inc(sum2_done, 1)

            def variance2(gg):
                dve.wait_ge(squared2, gg + 1)
                if not (known(gg) and gg == 0):
                    dve.wait_ge(norm2, gg)
                nc.vector.tensor_scalar(var2e[:, :], var2[:, :], 1.0 / HD, LN2_EPS, ALU.mult, ALU.add)\
                    .then_inc(var2_done, 1)

            dve.wait_ge(s_memset, 1)
            dve.wait_ge(s_id, 1)
            dve.wait_ge(s_vec, 48)
            stats(0)
            shifts(0)
            scale_factors(0)
            negate(0, 0)

            def body(b, first, last):
                for g in range(NG):
                    gg = b * NG + g
                    for p in range(NP):
                        if p == 0:
                            copy_mask(b, g, 0)
                        for u in range(NT):
                            if p == 0 and u + 1 < NT:
                                copy_mask(b, g, u + 1)
                            probs(b, g, p, u)
                            if p == 0 and u % CJ == CJ - 1:
                                check_adj(b, g, u // CJ)
                            if p == 0 and u == 14 and not (first and g == 0):
                                variance1(gg - 1)
                            if p == 1 and u == 11 and not (first and g == 0):
                                sum2(gg - 1, 1 - g)
                            if g == 0 and p == 0 and u == 15:
                                negate(b, 1)
                            if g == 1 and p == 1 and not last:
                                if u == 0:
                                    stats(b + 1)
                                if u == 1:
                                    shifts(b + 1)
                                if u == 3:
                                    scale_factors(b + 1)
                        finish_rows(b, g, p)
                        if p == 1 and not (first and g == 0):
                            variance2(gg - 1)
                    if g == 1 and not last:
                        negate(b + 1, 0)

            batches(dve, body)
            G = B * NG
            variance1(G - 1)
            sum2(G - 1, 1)
            variance2(G - 1)

        @block.tensor
        def _(pe):
            pe.wait_ge(s_const, 1)
            pe.wait_ge(s_w, 16 * (DC + 2))
            nc.tensor.transpose(pj[0:HO, 0:EC], a_rows, ident_f[0:EC, 0:EC])
            for c in range(DC):
                for h in range(H):
                    k = c * H + h
                    ins = nc.tensor.transpose(acc[k // 4][0:HO, (k % 4) * P:(k % 4 + 1) * P],
                                              w_cat[:, c, h * HO:(h + 1) * HO], ident_f[:, :])
            ins.then_inc(s_setup_pe, 1)
            pe.wait_ge(s_setup_act, 1)
            for c in range(DC):
                for h in range(H):
                    k = c * H + h
                    ins = nc.tensor.matmul(
                        acc[2][:, k * 2:(k + 1) * 2], wT[:, k, :],
                        aT.rearrange("p (k h) -> p k h", k=2)[:, :, h],
                        start=(k == 0), stop=True, skip_group_check=True)
            ins.then_inc(s_setup_pe, 1)

            def transpose_x(b, q):
                k = b * HALF + q
                pe.wait_ge(xp_loaded, 16 * (k + 1))
                if not (known(k) and k == 0):
                    pe.wait_ge(he_copied, 2 * k)
                for i in range(2):
                    for c in range(DC):
                        ins = nc.tensor.transpose(pj[:, (i * DC + c) * P:(i * DC + c + 1) * P],
                                                  x_pair[:, i, c * P:(c + 1) * P], ident_f[:, :])
                ins.then_inc(tx_done, 1)

            def project(b, q, i):
                k = b * HALF + q
                if i == 0:
                    pe.wait_ge(xt_copied, k + 1)
                else:
                    pe.wait_ge(he_copied, 2 * k + 1)
                for c in range(DC):
                    ins = nc.tensor.matmul(pj[:, 0:PW], xT[:, i, c, :], w_cat[:, c, :],
                                           start=(c == 0), stop=(c == DC - 1))
                ins.then_inc(mm_done, 1)

            def score_row(b):
                pe.wait_ge(st_vec, b + 1)
                pe.wait_ge(he_copied, NT * (b + 1))
                nc.tensor.transpose(pj[:, 0:P], s_hn[:, :, :].rearrange("p k n -> p (k n)"), ident_f[:, :])\
                    .then_inc(st_pe, 1)

            def transpose_mask(b, g, u):
                c = u // CJ
                jj = (b * NG + g) * NT + u
                if u % CJ == 0:
                    pe.wait_ge(adj_loaded[c % NCB], 16 * ((b * NG + g) * (NCG // NCB) + c // NCB + 1))
                if not (known(jj) and jj == 0):
                    pe.wait_ge(mask_copied, jj)
                for it in range(GI):
                    ins = nc.tensor.transpose(mT[:, it * P:(it + 1) * P],
                                              adj_b[:, c % NCB, it, (u % CJ) * P:(u % CJ + 1) * P], ident_b[:, :])
                ins.then_inc(mask_ready, 1)

            def products(b, g, p, u):
                uu = (b * NG + g) * UPG + p * NT + u
                if p == 0:
                    pe.wait_ge(mask_copied, (b * NG + g) * NT + u + 1)
                for it in range(GI):
                    for k in range(HP):
                        h = p * HP + k
                        for part in range(2):
                            nc.tensor.matmul(acc_of(it, k, "F"), mask[:, u, it * P:(it + 1) * P],
                                             rf[:, u, h, part, :], start=False, stop=False, skip_group_check=True)
                pe.wait_ge(b_ready, uu + 1)
                for it in range(GI):
                    for k in range(HP):
                        h = p * HP + k
                        for part in range(2):
                            ins = nc.tensor.matmul(acc_of(it, k), b_pos[:, u % 2, k, it * P:(it + 1) * P],
                                                   rh[:, u, h, part, :], start=False, stop=False,
                                                   skip_group_check=True)
                ins.then_inc(pv_done, 1)

            for q in range(HALF):
                transpose_x(0, q)
                project(0, q, 0)
                project(0, q, 1)
            score_row(0)

            def body(b, first, last):
                for g in range(NG):
                    for p in range(NP):
                        pp = (b * NG + g) * NP + p
                        if not (known(pp) and pp == 0):
                            pe.wait_ge(acc_out_act, pp)
                            pe.wait_ge(acc_out_dve, pp)
                        if g == 0:
                            pe.wait_ge(neg_done, b * NP + p + 1)
                        for k in range(NAB):
                            a, e = bank_pairs(k)
                            w = (e - a) * 2 * AW
                            nc.tensor.matmul(acc[k][:, 0:w], zeros[:, 0:P], zeros[:, 0:w], start=True, stop=True)
                        if p == 0:
                            transpose_mask(b, g, 0)
                        for u in range(NT):
                            if g == 1 and p == 0 and not last:
                                if u % 2 == 0:
                                    transpose_x(b + 1, u // 2)
                                else:
                                    project(b + 1, u // 2, 0)
                            if p == 0 and u + 1 < NT:
                                transpose_mask(b, g, u + 1)
                            products(b, g, p, u)
                            if g == 1 and p == 0 and not last and u % 2 == 1:
                                project(b + 1, u // 2, 1)
                            if g == 1 and p == 1 and not last and u == 0:
                                score_row(b + 1)

            batches(pe, body)


_INS = ['x', 'adj', 'L0_gnn_W', 'L0_gnn_a_src', 'L0_gnn_a_dst', 'L0_gnn_bias', 'L0_gnn_ln_gamma', 'L0_gnn_ln_beta']


def kernel(**inputs):
    import numpy as _np
    import concourse.bacc as _bacc
    from concourse import mybir as _mybir
    from concourse.bass_utils import run_bass_kernel_spmd as _run

    nc = _bacc.Bacc("TRN2", target_bir_lowering=False, num_devices=1)
    arrays, args = {}, []
    for name in _INS:
        a = _np.ascontiguousarray(inputs[name])
        arrays[f"in_{name}_dram"] = a
        args.append(nc.dram_tensor(f"in_{name}_dram", a.shape, _mybir.dt.from_np(a.dtype), kind="ExternalInput").ap())
    shape = inputs["x"].shape
    args.append(nc.dram_tensor("out_0_dram", shape, _mybir.dt.float32, kind="ExternalOutput").ap())
    nc.disable_value_cache = True
    gat_layer(nc, *args)
    r = _run(nc, [arrays], core_ids=[0])
    return r.results[0]["out_0_dram"]
```

```python
import concourse.bass as bass
from concourse import mybir
from contextlib import ExitStack

FP32 = mybir.dt.float32
BF16 = mybir.dt.bfloat16
I32 = mybir.dt.int32
FP16 = mybir.dt.float16
ALU = mybir.AluOpType
ACT = mybir.ActivationFunctionType
AX = mybir.AxisListType


def gat_layer(nc, x, adj, W, a_src, a_dst, bias, gamma, beta, out):
    B, N, D = x.shape
    H, _, HO = W.shape
    T = a_src.shape[1]
    P = 128
    NT = N // P
    GI = 8
    NG = NT // GI
    IW = GI * P
    HP = 2
    NP = H // HP
    CJ = 2
    NCB = 4
    NCG = NT // CJ
    DC = D // P
    HD = H * HO
    EC = 2 * H
    PW = HD + EC
    AW = HO + 1
    PERBANK = 512 // (2 * AW)
    NPAIR = GI * HP
    NAB = -(-NPAIR // PERBANK)
    LN1_EPS, LN2_EPS = 1e-6, 1e-5
    SLOPE = 0.01
    BIG = 1e30
    SCALE = 4096.0
    UPG = NP * NT

    ctx = ExitStack()
    with ctx:
        def sb(name, shape, dt=FP32):
            return ctx.enter_context(nc.sbuf_tensor(name, shape, dt))

        def pb(name, shape, dt=FP32):
            return ctx.enter_context(nc.psum_tensor(name, shape, dt))

        def sem(name):
            return ctx.enter_context(nc.semaphore(name))

        score_rows = nc.dram_tensor("score_rows", (2, H * NT, P), FP32, kind="Internal").ap()

        ident_b = sb("ident_b", [P, P], BF16)
        ident_f = sb("ident_f", [P, P])
        zeros = sb("zeros", [P, PERBANK * 2 * AW], BF16)
        w_cat = sb("w_cat", [P, DC, PW])
        bias_b = sb("bias_b", [P, HD])
        gamma_b = sb("gamma_b", [P, HD])
        beta_b = sb("beta_b", [P, HD])
        minus_half = sb("minus_half", [P, GI * H])
        adj_b = sb("adj_b", [P, NCB, GI, CJ * P], BF16)
        mask = sb("mask", [P, NT, IW], BF16)
        s_bc = sb("s_bc", [P, NP, HP, IW])
        he = sb("he", [P, NT + NT // 2, PW])
        rh = sb("rh", [P, NT, H, 2, 2 * AW], FP16)
        rf = sb("rf", [P, NT, H, 2, AW], FP16)
        v = sb("v", [P, NT, AW])
        d_big = sb("d_big", [P, 2, NT * H])
        fac = sb("fac", [P, 2, NT, H])
        g_fac = sb("g_fac", [P, 2, NT, H])
        r = sb("r", [P, 2, HP, IW], BF16)
        b_pos = sb("b_pos", [P, 2, HP, IW], BF16)
        x_pair = sb("x_pair", [P, 2, D])
        xT = sb("xT", [P, 2, DC, P])
        o = sb("o", [P, NPAIR, 2 * AW])
        y = sb("y", [P, NG, GI, HD])
        xr = sb("xr", [P, GI, HD])
        seen = sb("seen", [P, GI * CJ * P // 4], I32)
        wait_pad = sb("wait_pad", [P, 1])
        rden = sb("rden", [P, NPAIR])
        dmin = sb("dmin", [P, 2])
        mean1 = sb("mean1", [P, GI, H])
        var1 = sb("var1", [P, GI * H])
        rstd1 = sb("rstd1", [P, GI * H])
        mean2 = sb("mean2", [P, NG, GI])
        var2 = sb("var2", [P, GI])
        var2e = sb("var2e", [P, GI])
        rstd2 = sb("rstd2", [P, GI])
        nmr2 = sb("nmr2", [P, GI])
        dmax_l = sb("dmax_l", [P, H])
        dmax = sb("dmax", [P, H])
        d_sh = sb("d_sh", [P, NT, H])
        sg_sh = sb("sg_sh", [P, NT, H])
        s_hn = sb("s_hn", [P, 2, H * NT])
        sT = sb("sT", [P, P])
        eabs = sb("eabs", [P, 2])
        a_rows = y[0:2 * H, 0, 0, 0:HO]
        aT = y[0:HO, 0, 1, 0:EC]
        wT = y[0:HO, 1, :, 0:P]

        acc = [pb(f"acc{i}", [P, 512]) for i in range(NAB)]
        mT = pb("mT", [P, IW], BF16)
        pj = pb("pj", [P, 512])

        def acc_of(it, k, part=None):
            n = it * HP + k
            c = (n % PERBANK) * 2 * AW
            lo, hi = {None: (0, 2 * AW), "E": (0, AW), "F": (AW, 2 * AW)}[part]
            return acc[n // PERBANK][:, c + lo:c + hi]

        def bank_pairs(k):
            return PERBANK * k, min(PERBANK * (k + 1), NPAIR)

        ACT_BANKS = range(0, 4)
        DVE_BANKS = range(4, NAB)

        s_id = sem("s_id")
        s_const = sem("s_const")
        s_w = sem("s_w")
        s_vec = sem("s_vec")
        s_setup_pe = sem("s_setup_pe")
        s_setup_act = sem("s_setup_act")
        s_memset = sem("s_memset")
        adj_loaded = [sem(f"adj_loaded{c}") for c in range(NCB)]
        adj_checked = sem("adj_checked")
        mask_ready = sem("mask_ready")
        mask_copied = sem("mask_copied")
        r_ready = sem("r_ready")
        b_ready = sem("b_ready")
        pv_done = sem("pv_done")
        acc_out_act = sem("acc_out_act")
        acc_out_dve = sem("acc_out_dve")
        xp_loaded = sem("xp_loaded")
        tx_done = sem("tx_done")
        xt_copied = sem("xt_copied")
        mm_done = sem("mm_done")
        he_copied = sem("he_copied")
        stats_done = sem("stats_done")
        dmax_done = sem("dmax_done")
        pro_done = sem("pro_done")
        exps_done = sem("exps_done")
        fac_done = sem("fac_done")
        v_done = sem("v_done")
        hi_done = sem("hi_done")
        lo_done = sem("lo_done")
        neg_done = sem("neg_done")
        st_vec = sem("st_vec")
        st_pe = sem("st_pe")
        st_act = sem("st_act")
        rows_stored = sem("rows_stored")
        s_loaded = [sem(f"s_loaded{p}") for p in range(NP)]
        y_chain = sem("y_chain")
        centred = sem("centred")
        squared1 = sem("squared1")
        var1_done = sem("var1_done")
        norm1 = sem("norm1")
        xr_loaded = sem("xr_loaded")
        sum2_done = sem("sum2_done")
        squared2 = sem("squared2")
        var2_done = sem("var2_done")
        norm2 = sem("norm2")
        pool_chain1 = sem("pool_chain1")
        pool_chain2 = sem("pool_chain2")
        stored = [sem(f"stored{g}") for g in range(NG)]

        YK = 9
        SK = 2
        ITEM_AT = (7, 9, 11, 13)
        NITEM = 2 * HP
        HALF = NT // 2

        block = ctx.enter_context(nc.Block())

        def known(*counts):
            return all(isinstance(n, int) for n in counts)

        def batches(eng, body):
            body(0, True, B == 1)
            if B > 2:
                with eng.Fori(1, B - 1) as b:
                    body(b, False, False)
            if B > 1:
                body(B - 1, False, True)

        def he_rows(b, t, n=1):
            if isinstance(t, int) and t < HALF:
                return bass.ds(t, n)
            return bass.ds(HALF + (b % 2) * HALF + (t - HALF), n)

        PAIR_ORDER = tuple(range(HALF // 2, HALF)) + tuple(range(HALF // 2))
        halves = ((0, HALF), (HALF, HALF))

        @block.sync
        def _(sp):
            for c in range(DC):
                sp.dma_start(w_cat[:, c, 0:HD].rearrange("p (h e) -> p h e", h=H),
                             W[:, c * P:(c + 1) * P, :].rearrange("h p e -> p h e")).then_inc(s_w, 16)
            sp.dma_start(a_rows[0:H, :], a_src[:, 0, :]).then_inc(s_w, 16)
            sp.dma_start(a_rows[H:EC, :], a_dst[:, 0, :]).then_inc(s_w, 16)
            for dst, src in ((bias_b, bias), (gamma_b, gamma), (beta_b, beta)):
                sp.dma_start(dst[:, :], src.rearrange("(o h) e -> o (h e)", o=1).to_broadcast((P, HD)))\
                  .then_inc(s_vec, 16)

            def load_pair(b, i):
                k, q = b * HALF + i, PAIR_ORDER[i]
                if not (known(k) and k == 0):
                    sp.wait_ge(tx_done, k)
                sp.dma_start(x_pair[:, :, :],
                             x[b, bass.ds(q * 2 * P, 2 * P), :].rearrange("(t p) d -> p t d", p=P))\
                  .then_inc(xp_loaded, 16)

            def load_scores(b, g, p):
                gg = b * NG + g
                if not (known(gg) and gg == 0):
                    sp.wait_ge(r_ready, HP * ((gg - 1) * UPG + (p + 1) * NT))
                sp.dma_start(s_bc[:, p, :, :],
                             score_rows[b % 2, :, :].rearrange("(o h t) n -> o h (t n)", o=1, h=H)
                             [:, p * HP:(p + 1) * HP, g * IW:(g + 1) * IW].to_broadcast((P, HP, IW)))\
                  .then_inc(s_loaded[p], 16)

            def store_rows(b):
                sp.wait_ge(st_act, b + 1)
                sp.dma_start(score_rows[b % 2, :, :], sT[0:H * NT, :]).then_inc(rows_stored, 16)
                sp.wait_ge(rows_stored, (b + 1) * 16)

            def load_xr(gg, b, g):
                if not (known(gg) and gg == 0):
                    sp.wait_ge(norm1, gg)
                sp.dma_start(xr[:, :, :], x[b, g * IW:(g + 1) * IW, :].rearrange("(t p) d -> p t d", p=P))\
                  .then_inc(xr_loaded, 16)

            def store_out(gg, b, g):
                sp.wait_ge(norm2, gg + 1)
                sp.dma_start(out[b, g * IW:(g + 1) * IW, :].rearrange("(t p) d -> p t d", p=P),
                             y[:, g, :, :]).then_inc(stored[g], 16)

            sp.wait_ge(s_setup_act, 2)
            for i in range(HALF):
                load_pair(0, i)
            store_rows(0)
            load_scores(0, 0, 0)
            load_scores(0, 0, 1)

            def body(b, first, last):
                gg = b * NG
                if not first:
                    load_xr(gg - 1, b - 1, 1)
                if not first:
                    store_out(gg - 2, b - 1, 0)
                load_scores(b, 1, 0)
                load_scores(b, 1, 1)
                load_xr(gg, b, 0)
                for q in range(HALF):
                    if not last:
                        load_pair(b + 1, q)
                    if q == 5 and not first:
                        store_out(gg - 1, b - 1, 1)
                if not last:
                    store_rows(b + 1)
                    load_scores(b + 1, 0, 0)
                    load_scores(b + 1, 0, 1)

            batches(sp, body)
            load_xr(B * NG - 1, B - 1, 1)
            store_out(B * NG - 2, B - 1, 0)
            store_out(B * NG - 1, B - 1, 1)
            for g in range(NG):
                sp.wait_ge(stored[g], 16 * B)

        @block.gpsimd
        def _(pool):
            nc.gpsimd.memset(ident_b[:, :], 0.0)
            nc.gpsimd.memset(ident_f[:, :], 0.0)
            nc.gpsimd.memset(minus_half[:, :], -0.5)
            nc.gpsimd.memset(zeros[:, :], 0.0)
            nc.gpsimd.memset(seen[:, :], 0).then_inc(s_id, 1)
            pool.wait_ge(s_id, 1)
            for m in (ident_b, ident_f):
                last_ins = nc.gpsimd.affine_select(out=m[:, :], in_=m[:, :], compare_op=ALU.not_equal,
                                                   fill=1.0, base=0, pattern=[[-1, P]],
                                                   channel_multiplier=1)
            last_ins.then_inc(s_const, 1)
            pool.wait_ge(s_const, 1)

            def load_adj(b, g, c):
                gg = b * NG + g
                if not (known(gg) and gg == 0 and c < NCB):
                    n = gg * NCG + c - NCB
                    pool.wait_ge(adj_checked, 2 * (n + 1))
                    pool.wait_ge(mask_ready, (n + 1) * CJ)
                j0 = c * CJ * P
                nc.gpsimd.dma_start(
                    adj_b[:, c % NCB, :, :],
                    adj[b, g * IW:(g + 1) * IW, j0:j0 + CJ * P].rearrange("(t p) j -> p t j", p=P))\
                    .then_inc(adj_loaded[c % NCB], 16)

            def next_group(b, g, last):
                if g + 1 < NG:
                    for c in range(NCB):
                        load_adj(b, g + 1, c)
                elif not last:
                    for c in range(NCB):
                        load_adj(b + 1, 0, c)

            for c in range(NCB):
                load_adj(0, 0, c)

            def max_of_all(b):
                pool.wait_ge(stats_done, SK * b + 1)
                nc.gpsimd.tensor_tensor(wait_pad[:, :], minus_half[:, 0:1], minus_half[:, 0:1], ALU.mult)
                nc.gpsimd.partition_all_reduce(dmax[:, :], dmax_l[:, :], P, bass.bass_isa.ReduceOp.max)\
                    .then_inc(dmax_done, 1)

            def centre(gg, g):
                pool.wait_ge(y_chain, YK * NP * (gg + 1))
                yv = y[:, g, :, :].rearrange("p t (h e) -> p (t h) e", h=H)
                nc.gpsimd.tensor_tensor(
                    yv, yv, mean1[:, :, :].rearrange("p t h -> p (t h)").unsqueeze(2).to_broadcast((P, GI * H, HO)),
                    ALU.subtract).then_inc(centred, 1)

            def normalise1(gg, g):
                n = 4 * gg
                pool.wait_ge(var1_done, 2 * gg + 2)
                nc.gpsimd.tensor_tensor(rstd1[:, :], var1[:, :], minus_half[:, :], ALU.pow).then_inc(pool_chain1, 1)
                pool.wait_ge(pool_chain1, n + 1)
                yh = y[:, g, :, :].rearrange("p t (h e) -> p (t h) e", h=H)
                nc.gpsimd.tensor_tensor(yh, yh, rstd1[:, :].unsqueeze(2).to_broadcast((P, GI * H, HO)),
                                        ALU.mult).then_inc(pool_chain1, 1)
                pool.wait_ge(pool_chain1, n + 2)
                yt = y[:, g, :, :]
                nc.gpsimd.tensor_tensor(yt, yt, gamma_b[:, :].unsqueeze(1).to_broadcast((P, GI, HD)),
                                        ALU.mult).then_inc(pool_chain1, 1)
                pool.wait_ge(pool_chain1, n + 3)
                nc.gpsimd.tensor_tensor(yt, yt, beta_b[:, :].unsqueeze(1).to_broadcast((P, GI, HD)),
                                        ALU.add).then_inc(pool_chain1, 1)
                pool.wait_ge(pool_chain1, n + 4)
                pool.wait_ge(xr_loaded, 16 * (gg + 1))
                nc.gpsimd.tensor_tensor(yt, yt, xr[:, :, :], ALU.add).then_inc(norm1, 1)

            def normalise2(gg, g):
                n = 3 * gg
                pool.wait_ge(var2_done, gg + 1)
                nc.gpsimd.tensor_tensor(rstd2[:, :], var2e[:, :], minus_half[:, 0:GI], ALU.pow)\
                    .then_inc(pool_chain2, 1)
                pool.wait_ge(pool_chain2, n + 1)
                nc.gpsimd.tensor_tensor(nmr2[:, :], mean2[:, g, :], rstd2[:, :], ALU.mult)\
                    .then_inc(pool_chain2, 1)
                pool.wait_ge(pool_chain2, n + 2)
                yt = y[:, g, :, :]
                nc.gpsimd.tensor_tensor(yt, yt, rstd2[:, :].unsqueeze(2).to_broadcast((P, GI, HD)), ALU.mult)\
                    .then_inc(pool_chain2, 1)
                pool.wait_ge(pool_chain2, n + 3)
                nc.gpsimd.tensor_tensor(yt, yt, nmr2[:, :].unsqueeze(2).to_broadcast((P, GI, HD)), ALU.add)\
                    .then_inc(norm2, 1)

            max_of_all(0)

            def body(b, first, last):
                for g in range(NG):
                    gg = b * NG + g
                    for c in range(NCB, NCG):
                        load_adj(b, g, c)
                    if not (first and g == 0):
                        centre(gg - 1, 1 - g)
                    if not first:
                        normalise2(gg - 2, g)
                    next_group(b, g, last)
                    if g == NG - 1 and not last:
                        max_of_all(b + 1)
                    if not (first and g == 0):
                        normalise1(gg - 1, 1 - g)

            batches(pool, body)
            G = B * NG
            centre(G - 1, 1)
            normalise2(G - 2, 0)
            normalise1(G - 1, 1)
            normalise2(G - 1, 1)

        @block.scalar
        def _(act):
            act.wait_ge(s_setup_pe, 1)
            nc.scalar.activation(aT, pj[0:HO, 0:EC], ACT.Copy)
            nc.scalar.activation(wT[:, 0:4, :], acc[0][0:HO, :].rearrange("p (k n) -> p k n", n=P), ACT.Copy)
            nc.scalar.activation(wT[:, 4:8, :], acc[1][0:HO, :].rearrange("p (k n) -> p k n", n=P), ACT.Copy)\
                .then_inc(s_setup_act, 1)
            act.wait_ge(s_setup_pe, 2)
            nc.scalar.activation(w_cat[:, :, HD:PW].rearrange("p c (k h) -> p c k h", k=2),
                                 acc[2][:, 0:DC * EC].rearrange("p (c h k) -> p c k h", c=DC, k=2), ACT.Copy)\
                .then_inc(s_setup_act, 1)

            def copy_xT(b, q):
                k = b * HALF + q
                act.wait_ge(tx_done, k + 1)
                if not (known(k) and k == 0):
                    act.wait_ge(mm_done, 2 * k)
                nc.scalar.activation(xT[:, :, :, :], pj[:, :].rearrange("p (a c n) -> p a c n", a=2, c=DC),
                                     ACT.Copy).then_inc(xt_copied, 1)

            def copy_he(b, n, i):
                k = b * HALF + n
                slots = he_rows(b, 2 * PAIR_ORDER[n] + i)
                act.wait_ge(mm_done, 2 * k + i + 1)
                if n == HALF // 2 and i == 0 and not (known(b) and b == 0):
                    act.wait_ge(y_chain, YK * ((b - 1) * NG * NP + 1) + 7)
                nc.scalar.activation(he[:, slots, :], pj[:, 0:PW].unsqueeze(1), ACT.Copy)\
                    .then_inc(he_copied, 1)

            def factors(b):
                act.wait_ge(pro_done, b + 1)
                nc.scalar.activation(fac[:, 0, :, :], d_sh[:, :, :], ACT.Exp)
                nc.scalar.activation(fac[:, 1, :, :], d_sh[:, :, :], ACT.Exp, scale=SLOPE)
                nc.scalar.activation(g_fac[:, bass.ds(b % 2, 1), :, :].rearrange("p o t h -> p (o t) h"),
                                     sg_sh[:, :, :], ACT.Exp, scale=SLOPE - 1.0).then_inc(exps_done, 1)

            def rows(b):
                act.wait_ge(st_pe, b + 1)
                if not (known(b) and b == 0):
                    act.wait_ge(rows_stored, 16 * b)
                nc.scalar.activation(sT[:, :], pj[:, 0:P], ACT.Copy).then_inc(st_act, 1)

            def high_part(b, p, m):
                n = (b * NP + p) * NITEM + m
                h, f = p * HP + m // 2, m % 2
                act.wait_ge(v_done, n + 1)
                if m == 0 and not (known(b) and b == 0):
                    act.wait_ge(pv_done, (b * NG - 1) * UPG + (p + 1) * NT)
                part = (rh[:, :, h, :, 0:AW], rf[:, :, h, :, :])[f]
                nc.scalar.activation(part[:, :, 0, :], v[:, :, :], ACT.Copy).then_inc(hi_done, 1)

            def positive(b, g, p, u, k):
                uu = (b * NG + g) * UPG + p * NT + u
                if u == 0 and k == 0:
                    act.wait_ge(s_loaded[p], 16 * (b * NG + g + 1))
                    act.wait_ge(pro_done, b + 1)
                if k == 0 and not (known(uu) and uu < 2):
                    act.wait_ge(b_ready, uu - 1)
                col = u * H + p * HP + k
                bias_ap = d_big[:, bass.ds(b % 2, 1), col:col + 1].rearrange("p o c -> p (o c)")
                nc.scalar.activation(r[:, u % 2, k, :], s_bc[:, p, k, :], ACT.Relu, bias=bias_ap, scale=BIG)\
                    .then_inc(r_ready, 1)

            def square1(gg, g):
                act.wait_ge(centred, gg + 1)
                if not (known(gg) and gg == 0):
                    act.wait_ge(squared2, gg)
                nc.scalar.activation(o_flat.rearrange("p (t e) -> p t e", e=HO),
                                     y[:, g, :, :].rearrange("p t (h e) -> p (t h) e", h=H),
                                     ACT.Square).then_inc(squared1, 1)

            o_flat = o[:, :, :].rearrange("p n w -> p (n w)")[:, 0:GI * HD]

            def square2(gg, g, steps):
                act.wait_ge(sum2_done, 2 * gg + 2)
                act.wait_ge(y_chain, steps)
                if not (known(gg) and gg == 0):
                    act.wait_ge(var2_done, gg)
                for it in range(GI):
                    ins = nc.scalar.activation(o_flat[:, it * HD:(it + 1) * HD], y[:, g, it, :], ACT.Square,
                                               bias=mean2[:, g, it:it + 1], accum_out=var2[:, it:it + 1])
                ins.then_inc(squared2, 1)

            def acc_out(b, g, p):
                pp = (b * NG + g) * NP + p
                act.wait_ge(pv_done, (pp + 1) * NT)
                if p == 0:
                    if not (known(pp) and pp == 0):
                        act.wait_ge(var1_done, 2 * (b * NG + g))
                        act.wait_ge(y_chain, YK * pp)
                else:
                    act.wait_ge(y_chain, YK * pp)
                for k in ACT_BANKS:
                    a, e = bank_pairs(k)
                    nc.scalar.activation(o[:, a:e, :].rearrange("p n w -> p (n w)"),
                                         acc[k][:, 0:(e - a) * 2 * AW], ACT.Copy).then_inc(acc_out_act, 1)

            for q in range(HALF):
                copy_xT(0, q)
                for i in range(2):
                    copy_he(0, q, i)
            factors(0)
            rows(0)
            for m in range(NITEM):
                high_part(0, 0, m)

            def body(b, first, last):
                for g in range(NG):
                    gg = b * NG + g
                    for p in range(NP):
                        for u in range(NT):
                            for k in range(HP):
                                positive(b, g, p, u, k)
                                if g == 1 and p == 0 and not last:
                                    q, step = u // 2, (u % 2) * 2 + k
                                    if step == 1:
                                        copy_xT(b + 1, q)
                                    if step == 2:
                                        copy_he(b + 1, q, 0)
                                    if step == 3:
                                        copy_he(b + 1, q, 1)
                            if p == 0 and u == 13 and not (first and g == 0):
                                square1(gg - 1, 1 - g)
                            if p == 1 and u == 14 and not (first and g == 0):
                                square2(gg - 1, 1 - g, YK * (gg * NP + 1))
                            if g == 0 and p == 0 and u - 1 in ITEM_AT:
                                high_part(b, 1, ITEM_AT.index(u - 1))
                            if g == 1 and p == 1 and not last:
                                if u == 4:
                                    rows(b + 1)
                                    factors(b + 1)
                                if u - 1 in ITEM_AT:
                                    high_part(b + 1, 0, ITEM_AT.index(u - 1))
                        acc_out(b, g, p)

            batches(act, body)
            G = B * NG
            square1(G - 1, 1)
            square2(G - 1, 1, YK * G * NP)

        @block.vector
        def _(dve):
            nc.vector.memset(eabs[:, :], 0.0)
            nc.vector.memset(dmin[:, :], 1.0).then_inc(s_memset, 1)

            def stats(b):
                dve.wait_ge(he_copied, NT * (b + 1))
                if not (known(b) and b == 0):
                    dve.wait_ge(dmax_done, b)
                    dve.wait_ge(st_pe, b)
                for t, m in halves:
                    rows_ = he[:, he_rows(b, t, m), :]
                    nc.vector.tensor_copy(s_hn[:, 0, :].rearrange("p (h t) -> p t h", h=H)[:, t:t + m, :],
                                          rows_[:, :, HD:HD + H])
                    ins = nc.vector.tensor_copy(s_hn[:, 1, :].rearrange("p (h t) -> p t h", h=H)[:, t:t + m, :],
                                                rows_[:, :, HD + H:PW])
                ins.then_inc(st_vec, 1)
                dve.wait_ge(st_vec, b + 1)
                nc.vector.tensor_reduce(dmax_l[:, :], s_hn[:, 1, :].rearrange("p (h t) -> p h t", h=H), AX.X, ALU.max)\
                    .then_inc(stats_done, 1)
                nc.vector.tensor_reduce(eabs[:, 1:2], s_hn[:, :, :].rearrange("p k n -> p (k n)"), AX.X, ALU.max,
                                        apply_absolute_value=True).then_inc(stats_done, 1)

            def shifts(b):
                dve.wait_ge(stats_done, SK * b + 2)
                nc.vector.tensor_tensor(eabs[:, 0:1], eabs[:, 0:1], eabs[:, 1:2], ALU.max)
                nc.vector.tensor_scalar(d_big[:, bass.ds(b % 2, 1), :].rearrange("p o (t h) -> p (o h) t", h=H),
                                        s_hn[:, 1, :].rearrange("p (h t) -> p h t", h=H), BIG, None, ALU.mult)
                dve.wait_ge(dmax_done, b + 1)
                if not (known(b) and b == 0):
                    dve.wait_ge(exps_done, b)
                gmax = dmax[:, :].unsqueeze(1).to_broadcast((P, NT, H))
                nc.vector.tensor_tensor(sg_sh[:, :, :], s_hn[:, 0, :].rearrange("p (h t) -> p t h", h=H), gmax, ALU.add)
                nc.vector.tensor_tensor(d_sh[:, :, :], s_hn[:, 1, :].rearrange("p (h t) -> p t h", h=H), gmax,
                                        ALU.subtract).then_inc(pro_done, 1)

            def scale_factors(b):
                dve.wait_ge(exps_done, b + 1)
                ff = fac[:, :, :, :].rearrange("p f t h -> p (f t h)")
                nc.vector.tensor_scalar(ff, ff, SCALE, None, ALU.mult).then_inc(fac_done, 1)

            def negate(b, p):
                dve.wait_ge(lo_done, (b * NP + p + 1) * NITEM)
                for k in range(HP):
                    h = p * HP + k
                    for part in range(2):
                        ins = nc.vector.tensor_scalar(rh[:, :, h, part, AW:2 * AW], rf[:, :, h, part, :], -1.0, None,
                                                      ALU.mult)
                ins.then_inc(neg_done, 1)

            def copy_mask(b, g, u):
                jj = (b * NG + g) * NT + u
                dve.wait_ge(mask_ready, jj + 1)
                if not (known(b, g) and b == 0 and g == 0):
                    dve.wait_ge(pv_done, (b * NG + g - 1) * UPG + NT + u + 1)
                nc.vector.tensor_copy(mask[:, u, :], mT[:, :]).then_inc(mask_copied, 1)

            def probs(b, g, p, u):
                uu = (b * NG + g) * UPG + p * NT + u
                if p == 0:
                    dve.wait_ge(mask_copied, (b * NG + g) * NT + u + 1)
                dve.wait_ge(r_ready, HP * (uu + 1))
                if not (known(uu) and uu < 2):
                    dve.wait_ge(pv_done, uu - 1)
                nc.vector.tensor_tensor(b_pos[:, u % 2, :, :], r[:, u % 2, :, :],
                                        mask[:, u, :].unsqueeze(1).to_broadcast((P, HP, IW)), ALU.min)\
                    .then_inc(b_ready, 1)

            def check_adj(b, g, c):
                n = (b * NG + g) * NCG + c
                dve.wait_ge(adj_loaded[c % NCB], 16 * ((b * NG + g) * (NCG // NCB) + c // NCB + 1))
                bits = adj_b[:, c % NCB, :, :].rearrange("p t j -> p (t j)").bitcast(I32)
                w = GI * CJ * P // 4
                for i in range(2):
                    if not (known(n) and n == 0 and i == 0):
                        dve.wait_ge(adj_checked, 2 * n + i)
                    nc.vector.tensor_tensor(seen[:, :], seen[:, :], bits[:, i * w:(i + 1) * w],
                                            ALU.bitwise_or).then_inc(adj_checked, 1)

            def item_values(b, p, m):
                h, f = p * HP + m // 2, m % 2
                n = (b * NP + p) * NITEM + m
                dve.wait_ge(fac_done, b + 1)
                if not (known(n) and n == 0):
                    dve.wait_ge(lo_done, n)
                for t, w in halves:
                    nc.vector.tensor_tensor(
                        v[:, t:t + w, 0:HO], he[:, he_rows(b, t, w), h * HO:(h + 1) * HO],
                        fac[:, f, t:t + w, h:h + 1].to_broadcast((P, w, HO)), ALU.mult)
                nc.vector.tensor_copy(v[:, :, HO:AW], fac[:, f, :, h:h + 1]).then_inc(v_done, 1)

            def item_low(b, p, m):
                h, f = p * HP + m // 2, m % 2
                dve.wait_ge(hi_done, (b * NP + p) * NITEM + m + 1)
                part = (rh[:, :, h, :, 0:AW], rf[:, :, h, :, :])[f]
                nc.vector.tensor_tensor(part[:, :, 1, :], v[:, :, :], part[:, :, 0, :], ALU.subtract)\
                    .then_inc(lo_done, 1)

            def build(b, p, u):
                if u - 2 in ITEM_AT:
                    item_low(b, p, ITEM_AT.index(u - 2))
                if u in ITEM_AT:
                    item_values(b, p, ITEM_AT.index(u))
                if u == ITEM_AT[-1] + 2:
                    negate(b, p)

            def acc_out(b, g, p):
                pp = (b * NG + g) * NP + p
                gg = b * NG + g
                dve.wait_ge(pv_done, (pp + 1) * NT)
                if not (known(pp) and pp <= 1):
                    if p == 0:
                        dve.wait_ge(var1_done, 2 * gg)
                    else:
                        dve.wait_ge(squared2, gg)
                for k in DVE_BANKS:
                    a, e = bank_pairs(k)
                    nc.vector.tensor_copy(o[:, a:e, :].rearrange("p n w -> p (n w)"),
                                          acc[k][:, 0:(e - a) * 2 * AW]).then_inc(acc_out_dve, 1)

            def finish(b, g, p, step):
                pp = (b * NG + g) * NP + p
                gg = b * NG + g
                n = YK * pp
                cols = slice(p * HP * HO, (p + 1) * HP * HO)
                yt = y[:, g, :, cols]
                yh = yt.rearrange("p t (h e) -> p t h e", h=HP)
                oh = o[:, :, :].rearrange("p (t h) w -> p t h w", h=HP)
                den = o[:, :, HO:AW].rearrange("p n o -> p (n o)")
                m1 = mean1[:, :, p * HP:(p + 1) * HP]
                if step == 0:
                    dve.wait_ge(acc_out_dve, len(DVE_BANKS) * (pp + 1))
                    dve.wait_ge(acc_out_act, len(ACT_BANKS) * (pp + 1))
                    gsc = g_fac[:, bass.ds(b % 2, 1), g * GI:(g + 1) * GI, p * HP:(p + 1) * HP]\
                        .rearrange("p o t h -> p (o t) h").unsqueeze(3).to_broadcast((P, GI, HP, AW))
                    nc.vector.tensor_tensor(oh[:, :, :, AW:2 * AW], oh[:, :, :, AW:2 * AW], gsc, ALU.mult)\
                        .then_inc(y_chain, 1)
                if step == 1:
                    dve.wait_ge(y_chain, n + 1)
                    nc.vector.tensor_tensor(o[:, :, 0:AW], o[:, :, 0:AW], o[:, :, AW:2 * AW], ALU.add)\
                        .then_inc(y_chain, 1)
                if step == 2:
                    dve.wait_ge(y_chain, n + 2)
                    nc.vector.tensor_reduce(dmin[:, 1:2], den, AX.X, ALU.min).then_inc(y_chain, 1)
                    nc.vector.reciprocal(rden[:, :], den).then_inc(y_chain, 1)
                if step == 3:
                    dve.wait_ge(y_chain, n + 4)
                    nc.vector.tensor_tensor(dmin[:, 0:1], dmin[:, 0:1], dmin[:, 1:2], ALU.min)
                    if p == 0 and not (known(gg) and gg < NG):
                        dve.wait_ge(stored[g], 16 * b)
                    nc.vector.tensor_tensor(yh, oh[:, :, :, 0:HO],
                                            rden[:, :].rearrange("p (t h) -> p t h", h=HP).unsqueeze(3)
                                            .to_broadcast((P, GI, HP, HO)), ALU.mult).then_inc(y_chain, 1)
                if step == 4:
                    dve.wait_ge(y_chain, n + 5)
                    nc.vector.tensor_tensor(yt, yt, bias_b[:, cols].unsqueeze(1).to_broadcast((P, GI, HP * HO)),
                                            ALU.add).then_inc(y_chain, 1)
                if step == 5:
                    dve.wait_ge(y_chain, n + 6)
                    nc.vector.scalar_tensor_tensor(yt, yt, 0.0, he[:, he_rows(b, g * GI, GI), cols],
                                                   ALU.max, ALU.add).then_inc(y_chain, 1)
                if step == 6:
                    dve.wait_ge(y_chain, n + 7)
                    if p == 0 and not (known(gg) and gg == 0):
                        dve.wait_ge(centred, gg)
                    nc.vector.tensor_reduce(m1, yh, AX.X, ALU.add).then_inc(y_chain, 1)
                if step == 7:
                    dve.wait_ge(y_chain, n + 8)
                    nc.vector.tensor_scalar(m1, m1, 1.0 / HO, None, ALU.mult).then_inc(y_chain, 1)

            def variance1(gg):
                dve.wait_ge(squared1, gg + 1)
                if not (known(gg) and gg == 0):
                    dve.wait_ge(norm1, gg)
                nc.vector.tensor_reduce(var1[:, :], o[:, :, :].rearrange("p n w -> p (n w)")[:, 0:GI * HD]
                                        .rearrange("p (t e) -> p t e", e=HO), AX.X, ALU.add).then_inc(var1_done, 1)
                dve.wait_ge(var1_done, 2 * gg + 1)
                nc.vector.tensor_scalar(var1[:, :], var1[:, :], 1.0 / HO, LN1_EPS, ALU.mult, ALU.add)\
                    .then_inc(var1_done, 1)

            def sum2(gg, g):
                dve.wait_ge(norm1, gg + 1)
                nc.vector.tensor_reduce(mean2[:, g, :], y[:, g, :, :], AX.X, ALU.add).then_inc(sum2_done, 1)
                dve.wait_ge(sum2_done, 2 * gg + 1)
                nc.vector.tensor_scalar(mean2[:, g, :], mean2[:, g, :], -1.0 / HD, None, ALU.mult)\
                    .then_inc(sum2_done, 1)

            def variance2(gg):
                dve.wait_ge(squared2, gg + 1)
                if not (known(gg) and gg == 0):
                    dve.wait_ge(norm2, gg)
                nc.vector.tensor_scalar(var2e[:, :], var2[:, :], 1.0 / HD, LN2_EPS, ALU.mult, ALU.add)\
                    .then_inc(var2_done, 1)

            dve.wait_ge(s_memset, 1)
            dve.wait_ge(s_id, 1)
            dve.wait_ge(s_vec, 48)
            stats(0)
            shifts(0)
            scale_factors(0)
            for m in range(NITEM):
                item_values(0, 0, m)
                item_low(0, 0, m)
            negate(0, 0)

            def body(b, first, last):
                for g in range(NG):
                    gg = b * NG + g
                    for p in range(NP):
                        pp = gg * NP + p
                        before = (b, g, 0) if p else (b, 0, 1) if g else (b - 1, 1, 1)
                        if first and g == 0 and p == 0:
                            before = None
                            copy_mask(b, g, 0)
                            copy_mask(b, g, 1)
                        for u in range(NT):
                            probs(b, g, p, u)
                            if u == 0 and before:
                                acc_out(*before)
                            elif before and u <= 8:
                                finish(*before, u - 1)
                            if p == 0:
                                if u + 2 < NT:
                                    copy_mask(b, g, u + 2)
                                if u % CJ == CJ - 1:
                                    check_adj(b, g, u // CJ)
                                if u == 15 and before:
                                    variance1(gg - 1)
                            else:
                                if u == 12 and not (first and g == 0):
                                    sum2(gg - 1, 1 - g)
                                if u >= NT - 2 and not (last and g == NG - 1):
                                    copy_mask(*((b, g + 1) if g + 1 < NG else (b + 1, 0)), u + 2 - NT)
                                if u == 15 and not (first and g == 0):
                                    variance2(gg - 1)
                            if g == 0 and p == 0:
                                build(b, 1, u)
                            if g == 1 and p == 1 and not last:
                                if u == 1:
                                    stats(b + 1)
                                if u == 3:
                                    shifts(b + 1)
                                if u == 6:
                                    scale_factors(b + 1)
                                build(b + 1, 0, u)

            batches(dve, body)
            G = B * NG
            acc_out(B - 1, 1, 1)
            for step in range(8):
                finish(B - 1, 1, 1, step)
            variance1(G - 1)
            sum2(G - 1, 1)
            variance2(G - 1)

        @block.tensor
        def _(pe):
            pe.wait_ge(s_const, 1)
            pe.wait_ge(s_w, 16 * (DC + 2))
            nc.tensor.transpose(pj[0:HO, 0:EC], a_rows, ident_f[0:EC, 0:EC])
            for c in range(DC):
                for h in range(H):
                    k = c * H + h
                    ins = nc.tensor.transpose(acc[k // 4][0:HO, (k % 4) * P:(k % 4 + 1) * P],
                                              w_cat[:, c, h * HO:(h + 1) * HO], ident_f[:, :])
            ins.then_inc(s_setup_pe, 1)
            pe.wait_ge(s_setup_act, 1)
            for c in range(DC):
                for h in range(H):
                    k = c * H + h
                    ins = nc.tensor.matmul(
                        acc[2][:, k * 2:(k + 1) * 2], wT[:, k, :],
                        aT.rearrange("p (k h) -> p k h", k=2)[:, :, h],
                        start=(k == 0), stop=True, skip_group_check=True)
            ins.then_inc(s_setup_pe, 1)

            def transpose_x(b, q):
                k = b * HALF + q
                pe.wait_ge(xp_loaded, 16 * (k + 1))
                if not (known(k) and k == 0):
                    pe.wait_ge(he_copied, 2 * k)
                for i in range(2):
                    for c in range(DC):
                        ins = nc.tensor.transpose(pj[:, (i * DC + c) * P:(i * DC + c + 1) * P],
                                                  x_pair[:, i, c * P:(c + 1) * P], ident_f[:, :])
                ins.then_inc(tx_done, 1)

            def project(b, q, i):
                k = b * HALF + q
                if i == 0:
                    pe.wait_ge(xt_copied, k + 1)
                else:
                    pe.wait_ge(he_copied, 2 * k + 1)
                for c in range(DC):
                    ins = nc.tensor.matmul(pj[:, 0:PW], xT[:, i, c, :], w_cat[:, c, :],
                                           start=(c == 0), stop=(c == DC - 1))
                ins.then_inc(mm_done, 1)

            def score_row(b):
                pe.wait_ge(st_vec, b + 1)
                pe.wait_ge(he_copied, NT * (b + 1))
                nc.tensor.transpose(pj[:, 0:P], s_hn[:, :, :].rearrange("p k n -> p (k n)"), ident_f[:, :])\
                    .then_inc(st_pe, 1)

            def transpose_mask(b, g, u):
                c = u // CJ
                jj = (b * NG + g) * NT + u
                if u % CJ == 0:
                    pe.wait_ge(adj_loaded[c % NCB], 16 * ((b * NG + g) * (NCG // NCB) + c // NCB + 1))
                if not (known(jj) and jj == 0):
                    pe.wait_ge(mask_copied, jj)
                for it in range(GI):
                    ins = nc.tensor.transpose(mT[:, it * P:(it + 1) * P],
                                              adj_b[:, c % NCB, it, (u % CJ) * P:(u % CJ + 1) * P], ident_b[:, :])
                ins.then_inc(mask_ready, 1)

            def products(b, g, p, u):
                uu = (b * NG + g) * UPG + p * NT + u
                if p == 0:
                    pe.wait_ge(mask_copied, (b * NG + g) * NT + u + 1)
                for it in range(GI):
                    for k in range(HP):
                        h = p * HP + k
                        for part in range(2):
                            nc.tensor.matmul(acc_of(it, k, "F"), mask[:, u, it * P:(it + 1) * P],
                                             rf[:, u, h, part, :], start=False, stop=False, skip_group_check=True)
                pe.wait_ge(b_ready, uu + 1)
                for it in range(GI):
                    for k in range(HP):
                        h = p * HP + k
                        for part in range(2):
                            ins = nc.tensor.matmul(acc_of(it, k), b_pos[:, u % 2, k, it * P:(it + 1) * P],
                                                   rh[:, u, h, part, :], start=False, stop=False,
                                                   skip_group_check=True)
                ins.then_inc(pv_done, 1)

            for q in range(HALF):
                transpose_x(0, q)
                project(0, q, 0)
                project(0, q, 1)
            score_row(0)

            def body(b, first, last):
                for g in range(NG):
                    for p in range(NP):
                        pp = (b * NG + g) * NP + p
                        if g == 0:
                            pe.wait_ge(neg_done, b * NP + p + 1)
                        for k in range(NAB):
                            a, e = bank_pairs(k)
                            w = (e - a) * 2 * AW
                            if not (known(pp) and pp == 0):
                                if k in ACT_BANKS:
                                    pe.wait_ge(acc_out_act, len(ACT_BANKS) * (pp - 1) + k + 1)
                                else:
                                    pe.wait_ge(acc_out_dve, len(DVE_BANKS) * (pp - 1) + k - DVE_BANKS[0] + 1)
                            nc.tensor.matmul(acc[k][:, 0:w], zeros[:, 0:P], zeros[:, 0:w], start=True, stop=True)
                        if first and g == 0 and p == 0:
                            transpose_mask(b, g, 0)
                            transpose_mask(b, g, 1)
                        for u in range(NT):
                            if g == 1 and p == 0 and not last:
                                if u % 2 == 0:
                                    transpose_x(b + 1, u // 2)
                                else:
                                    project(b + 1, u // 2, 0)
                            if p == 0 and u + 2 < NT:
                                transpose_mask(b, g, u + 2)
                            if p == 1 and u >= NT - 2 and not (last and g == NG - 1):
                                transpose_mask(*((b, g + 1) if g + 1 < NG else (b + 1, 0)), u + 2 - NT)
                            products(b, g, p, u)
                            if g == 1 and p == 0 and not last and u % 2 == 1:
                                project(b + 1, u // 2, 1)
                            if g == 1 and p == 1 and not last and u == 0:
                                score_row(b + 1)

            batches(pe, body)


_INS = ['x', 'adj', 'L0_gnn_W', 'L0_gnn_a_src', 'L0_gnn_a_dst', 'L0_gnn_bias', 'L0_gnn_ln_gamma', 'L0_gnn_ln_beta']


def kernel(**inputs):
    import numpy as _np
    import concourse.bacc as _bacc
    from concourse import mybir as _mybir
    from concourse.bass_utils import run_bass_kernel_spmd as _run

    nc = _bacc.Bacc("TRN2", target_bir_lowering=False, num_devices=1)
    arrays, args = {}, []
    for name in _INS:
        a = _np.ascontiguousarray(inputs[name])
        arrays[f"in_{name}_dram"] = a
        args.append(nc.dram_tensor(f"in_{name}_dram", a.shape, _mybir.dt.from_np(a.dtype), kind="ExternalInput").ap())
    shape = inputs["x"].shape
    args.append(nc.dram_tensor("out_0_dram", shape, _mybir.dt.float32, kind="ExternalOutput").ap())
    nc.disable_value_cache = True
    gat_layer(nc, *args)
    r = _run(nc, [arrays], core_ids=[0])
    return r.results[0]["out_0_dram"]
```

```python
import concourse.bass as bass
from concourse import mybir
from contextlib import ExitStack

FP32 = mybir.dt.float32
BF16 = mybir.dt.bfloat16
I32 = mybir.dt.int32
FP16 = mybir.dt.float16
ALU = mybir.AluOpType
ACT = mybir.ActivationFunctionType
AX = mybir.AxisListType


def gat_layer(nc, x, adj, W, a_src, a_dst, bias, gamma, beta, out):
    B, N, D = x.shape
    H, _, HO = W.shape
    T = a_src.shape[1]
    P = 128
    NT = N // P
    GI = 8
    NG = NT // GI
    IW = GI * P
    HP = 2
    NP = H // HP
    CJ = 2
    NCB = 4
    NCG = NT // CJ
    DC = D // P
    HD = H * HO
    EC = 2 * H
    PW = HD + EC
    AW = HO + 1
    PERBANK = 512 // (2 * AW)
    NPAIR = GI * HP
    NAB = -(-NPAIR // PERBANK)
    LN1_EPS, LN2_EPS = 1e-6, 1e-5
    SLOPE = 0.01
    BIG = 1e30
    SCALE = 4096.0
    UPG = NP * NT
    ALLC = 2 * H * T
    NEG = -1e9
    MAX_SCORE = 25.0
    MAX_SPREAD = 10.0
    MAX_VALUE = 15.5
    TINY = 1e-30
    ONES = 0x3F803F80

    ctx = ExitStack()
    with ctx:
        def sb(name, shape, dt=FP32):
            return ctx.enter_context(nc.sbuf_tensor(name, shape, dt))

        def pb(name, shape, dt=FP32):
            return ctx.enter_context(nc.psum_tensor(name, shape, dt))

        def sem(name):
            return ctx.enter_context(nc.semaphore(name))

        type_rows = nc.dram_tensor("type_rows", (H * T, N), FP32, kind="Internal").ap()
        score_rows = nc.dram_tensor("score_rows", (2, H * NT, P), FP32, kind="Internal").ap()

        ident_b = sb("ident_b", [P, P], BF16)
        ident_f = sb("ident_f", [P, P])
        zeros = sb("zeros", [P, PERBANK * 2 * AW], BF16)
        w_cat = sb("w_cat", [P, DC, PW])
        w_all = sb("w_all", [P, DC, ALLC])
        bias_b = sb("bias_b", [P, HD])
        gamma_b = sb("gamma_b", [P, HD])
        beta_b = sb("beta_b", [P, HD])
        ones = sb("ones", [P, 1])
        minus_half = sb("minus_half", [P, GI * H])
        adj_b = sb("adj_b", [P, NCB, GI, CJ * P], BF16)
        mask = sb("mask", [P, NT, IW], BF16)
        s_bc = sb("s_bc", [P, NP, HP, IW])
        he = sb("he", [P, NT + NT // 2, PW])
        rh = sb("rh", [P, NT, H, 2, 2 * AW], FP16)
        rf_flat = sb("rf_flat", [P, NT * H * 2 * AW], FP16)
        rf = rf_flat[:, :].rearrange("p (t h q w) -> p t h q w", t=NT, h=H, q=2)
        v_flat = sb("v_flat", [P, NT * AW])
        v = v_flat[:, :].rearrange("p (t w) -> p t w", t=NT)
        b_neg = v_flat[:, 0:IW].bitcast(BF16).rearrange("p (s n) -> p s n", s=2)
        d_big = sb("d_big", [P, 2, NT * H])
        fac = sb("fac", [P, 2, NT, H])
        g_fac = sb("g_fac", [P, 2, NT, H])
        r = sb("r", [P, 2, HP, IW], BF16)
        b_pos = sb("b_pos", [P, 2, HP, IW], BF16)
        x_pair = sb("x_pair", [P, 2, D])
        xT = sb("xT", [P, 2, DC, P])
        o = sb("o", [P, NPAIR, 2 * AW])
        y = sb("y", [P, NG, GI, HD])
        xr = sb("xr", [P, GI, HD])
        seen = sb("seen", [P, GI * CJ * P // 4], I32)
        wait_pad = sb("wait_pad", [P, 1])
        rden = sb("rden", [P, NPAIR])
        dmin = sb("dmin", [P, 2])
        mean1 = sb("mean1", [P, GI, H])
        var1 = sb("var1", [P, GI * H])
        rstd1 = sb("rstd1", [P, GI * H])
        mean2 = sb("mean2", [P, NG, GI])
        var2 = sb("var2", [P, GI])
        var2e = sb("var2e", [P, GI])
        rstd2 = sb("rstd2", [P, GI])
        nmr2 = sb("nmr2", [P, GI])
        dmax_l = sb("dmax_l", [P, H])
        dmax = sb("dmax", [P, H])
        d_sh = sb("d_sh", [P, NT, H])
        sg_sh = sb("sg_sh", [P, NT, H])
        s_hn = sb("s_hn", [P, 2, H * NT])
        sT = sb("sT", [P, P])
        eabs = sb("eabs", [P, 2])
        dlow = sb("dlow", [P, 2])
        habs = sb("habs", [P, 1])
        hmax = sb("hmax", [P, 1])
        fits = sb("fits", [P, 1])
        seen_any = o[:, :, :].rearrange("p n w -> p (n w)")[:, 0:GI * CJ * P // 4]
        habs_part = sb("habs_part", [P, 2, H])
        tests = sb("tests", [P, 5])
        step_pad = sb("step_pad", [P, 6])
        beyond = sb("beyond", [P, 1])
        flag = sb("flag", [1, 1], I32)
        a_rows = y[0:ALLC, 0, 0, 0:HO]
        aT = y[0:HO, 0, 1, 0:ALLC]
        wT = y[0:HO, 1, :, 0:P]

        acc = [pb(f"acc{i}", [P, 512]) for i in range(NAB)]
        mT = pb("mT", [P, IW], BF16)
        pj = pb("pj", [P, 512])

        def acc_of(it, k, part=None):
            n = it * HP + k
            c = (n % PERBANK) * 2 * AW
            lo, hi = {None: (0, 2 * AW), "E": (0, AW), "F": (AW, 2 * AW)}[part]
            return acc[n // PERBANK][:, c + lo:c + hi]

        def first_banks(q, i):
            return acc[(q % 2) * 2 + i]

        def bank_pairs(k):
            return PERBANK * k, min(PERBANK * (k + 1), NPAIR)

        ACT_BANKS = range(0, 3)
        DVE_BANKS = range(3, NAB)

        s_id = sem("s_id")
        s_const = sem("s_const")
        s_w = sem("s_w")
        s_vec = sem("s_vec")
        s_setup_pe = sem("s_setup_pe")
        s_setup_act = sem("s_setup_act")
        s_memset = sem("s_memset")
        adj_loaded = [sem(f"adj_loaded{c}") for c in range(NCB)]
        adj_checked = sem("adj_checked")
        mask_ready = sem("mask_ready")
        mask_copied = sem("mask_copied")
        r_ready = sem("r_ready")
        b_ready = sem("b_ready")
        neg_ready = sem("neg_ready")
        pv_done = sem("pv_done")
        bank_done = sem("bank_done")
        acc_out_act = sem("acc_out_act")
        acc_out_dve = sem("acc_out_dve")
        xp_loaded = sem("xp_loaded")
        tx_done = sem("tx_done")
        xt_copied = sem("xt_copied")
        mm_done = sem("mm_done")
        he_copied = sem("he_copied")
        stats_done = sem("stats_done")
        dmax_done = sem("dmax_done")
        pro_done = sem("pro_done")
        exps_done = sem("exps_done")
        fac_done = sem("fac_done")
        v_done = sem("v_done")
        hi_done = sem("hi_done")
        lo_done = sem("lo_done")
        neg_done = sem("neg_done")
        st_vec = sem("st_vec")
        st_pe = sem("st_pe")
        st_act = sem("st_act")
        rows_stored = sem("rows_stored")
        s_loaded = [sem(f"s_loaded{p}") for p in range(NP)]
        y_chain = sem("y_chain")
        centred = sem("centred")
        squared1 = sem("squared1")
        var1_done = sem("var1_done")
        norm1 = sem("norm1")
        xr_loaded = sem("xr_loaded")
        sum2_done = sem("sum2_done")
        squared2 = sem("squared2")
        var2_done = sem("var2_done")
        norm2 = sem("norm2")
        pool_chain1 = sem("pool_chain1")
        pool_chain2 = sem("pool_chain2")
        stored = [sem(f"stored{g}") for g in range(NG)]
        spread_seen = sem("spread_seen")
        sums_done = sem("sums_done")
        values_seen = sem("values_seen")
        last_pow = sem("last_pow")
        last_steps = sem("last_steps")
        tested = sem("tested")
        beyond_summed = sem("beyond_summed")
        flag_ready = sem("flag_ready")
        tile_projected = sem("tile_projected")
        x_tile_loaded = sem("x_tile_loaded")
        x_tile_transposed = sem("x_tile_transposed")
        x_tile_copied = sem("x_tile_copied")
        tile_products = sem("tile_products")
        type_row_stored = sem("type_row_stored")
        type_row_kept = sem("type_row_kept")
        type_rows_loaded = sem("type_rows_loaded")
        head_copied = sem("head_copied")
        head_done = sem("head_done")
        attention_done = sem("attention_done")
        batch_done = sem("batch_done")
        adj_tile_loaded = sem("adj_tile_loaded")
        weight_steps = sem("weight_steps")
        exp_done = sem("exp_done")
        exp_transposed = sem("exp_transposed")
        exp_copied = sem("exp_copied")
        attention_product = sem("attention_product")
        rest_loaded = sem("rest_loaded")
        row_steps = sem("row_steps")
        row_pow = sem("row_pow")
        row_pow_asked = sem("row_pow_asked")
        rows_final = sem("rows_final")
        inverse_done = sem("inverse_done")

        YK = 10
        SK = 2
        LOW_AT = ((9, 11, 13, 15), (8, 10, 13, 15))
        NITEM = 2 * HP
        HALF = NT // 2

        block = ctx.enter_context(nc.Block())

        def known(*counts):
            return all(isinstance(n, int) for n in counts)

        def batches(eng, body):
            body(0, True, B == 1)
            if B > 2:
                with eng.Fori(1, B - 1) as b:
                    body(b, False, False)
            if B > 1:
                body(B - 1, False, True)

        def he_rows(b, t, n=1):
            if isinstance(t, int) and t < HALF:
                return bass.ds(t, n)
            return bass.ds(HALF + (b % 2) * HALF + (t - HALF), n)

        PAIR_ORDER = tuple(range(HALF // 2, HALF)) + tuple(range(HALF // 2))
        halves = ((0, HALF), (HALF, HALF))
        STEPS = 3
        START = (NT, UPG + 5)

        def apart(g, p):
            return g == 0 and p == 1

        def projection_step(g, p, u, behind=0):
            for half, start in enumerate(START):
                n = g * UPG + p * NT + u - behind - start
                if 0 <= n < STEPS * HALF // 2:
                    return half * HALF // 2 + n // STEPS, n % STEPS
            return None


        g_rows = [mask[:, :, :].rearrange("p t n -> p (t n)").bitcast(FP32)[:, t * N:(t + 1) * N]
                  for t in range(T - 1)] + [r[:, :, :, :].rearrange("p a h n -> p (a h n)").bitcast(FP32)]
        g_adj = adj_b[:, :, :, :].rearrange("p c t n -> p (c t n)").bitcast(I32)[:, 0:N]
        g_tmp = rf_flat[:, 0:4 * N].bitcast(FP32)
        g_w, g_part = g_tmp[:, 0:N], g_tmp[:, N:2 * N]
        g_expT = b_pos[:, :, :, :].rearrange("p a h n -> p (a h n)").bitcast(FP32)\
            .rearrange("p (t n) -> p t n", t=NT)
        g_src = v[:, :, 0:H * T]
        g_head = o[:, :, 0:HO]
        g_dst_row = sT[0:H * T, :]
        g_y = y[:, :, :, :].rearrange("p g t e -> p (g t) e")
        g_s = rden[:, 0:T]
        g_max, g_sum, g_inv = rstd2[:, 0:1], rstd2[:, 1:2], rstd2[:, 2:3]
        WS = 3 * T + 4
        RS = 17

        def second_path(eng, program):
            eng.wait_ge(flag_ready, 1)
            needed = eng.value_load(flag[0:1, 0:1], min_val=0, max_val=P)
            with eng.If(needed > 0):
                program()

        @block.sync
        def _(sp):
            for c in range(DC):
                sp.dma_start(w_cat[:, c, 0:HD].rearrange("p (h e) -> p h e", h=H),
                             W[:, c * P:(c + 1) * P, :].rearrange("h p e -> p h e")).then_inc(s_w, 16)
            sp.dma_start(a_rows[0:H * T, :], a_src.rearrange("h t e -> (h t) e")).then_inc(s_w, 16)
            sp.dma_start(a_rows[H * T:ALLC, :], a_dst.rearrange("h t e -> (h t) e")).then_inc(s_w, 16)
            for dst, src in ((bias_b, bias), (gamma_b, gamma), (beta_b, beta)):
                sp.dma_start(dst[:, :], src.rearrange("(o h) e -> o (h e)", o=1).to_broadcast((P, HD)))\
                  .then_inc(s_vec, 16)

            def load_pair(b, i):
                k, q = b * HALF + i, PAIR_ORDER[i]
                if not (known(k) and k == 0):
                    sp.wait_ge(tx_done, k)
                sp.dma_start(x_pair[:, :, :],
                             x[b, bass.ds(q * 2 * P, 2 * P), :].rearrange("(t p) d -> p t d", p=P))\
                  .then_inc(xp_loaded, 16)

            def load_scores(b, g, p):
                gg = b * NG + g
                if not (known(gg) and gg == 0):
                    sp.wait_ge(r_ready, HP * ((gg - 1) * UPG + (p + 1) * NT))
                sp.dma_start(s_bc[:, p, :, :],
                             score_rows[b % 2, :, :].rearrange("(o h t) n -> o h (t n)", o=1, h=H)
                             [:, p * HP:(p + 1) * HP, g * IW:(g + 1) * IW].to_broadcast((P, HP, IW)))\
                  .then_inc(s_loaded[p], 16)

            def store_rows(b):
                sp.wait_ge(st_act, b + 1)
                sp.dma_start(score_rows[b % 2, :, :], sT[0:H * NT, :]).then_inc(rows_stored, 16)
                sp.wait_ge(rows_stored, (b + 1) * 16)

            def load_xr(gg, b, g):
                if not (known(gg) and gg == 0):
                    sp.wait_ge(norm1, gg)
                sp.dma_start(xr[:, :, :], x[b, g * IW:(g + 1) * IW, :].rearrange("(t p) d -> p t d", p=P))\
                  .then_inc(xr_loaded, 16)

            def store_out(gg, b, g):
                sp.wait_ge(norm2, gg + 1)
                sp.dma_start(out[b, g * IW:(g + 1) * IW, :].rearrange("(t p) d -> p t d", p=P),
                             y[:, g, :, :]).then_inc(stored[g], 16)

            sp.wait_ge(s_setup_act, 2)
            for i in range(HALF):
                load_pair(0, i)
            store_rows(0)
            load_scores(0, 0, 0)
            load_scores(0, 0, 1)

            def body(b, first, last):
                gg = b * NG
                if not first:
                    load_xr(gg - 1, b - 1, 1)
                if not first:
                    store_out(gg - 2, b - 1, 0)
                load_scores(b, 1, 0)
                if not last:
                    for q in range(HALF // 2):
                        load_pair(b + 1, q)
                load_scores(b, 1, 1)
                load_xr(gg, b, 0)
                for q in range(HALF // 2, HALF):
                    if not last:
                        load_pair(b + 1, q)
                    if q == 6 and not first:
                        store_out(gg - 1, b - 1, 1)
                if not last:
                    store_rows(b + 1)
                    load_scores(b + 1, 0, 0)
                    load_scores(b + 1, 0, 1)

            batches(sp, body)
            load_xr(B * NG - 1, B - 1, 1)
            store_out(B * NG - 2, B - 1, 0)
            store_out(B * NG - 1, B - 1, 1)
            for g in range(NG):
                sp.wait_ge(stored[g], 16 * B)

            def general():
                with sp.Fori(0, B) as b:
                    with sp.Fori(0, NT) as t:
                        k = b * NT + t
                        sp.wait_ge(batch_done, b + 1)
                        sp.wait_ge(tile_projected, k + 1)
                        sp.dma_start(x_pair[:, 0, :], x[b, bass.ds(t * P, P), :]).then_inc(x_tile_loaded, 16)
                        sp.wait_ge(tile_projected, k + 2)
                        sp.dma_start(type_rows[:, bass.ds(t * P, P)], g_dst_row).then_inc(type_row_stored, 16)
                        sp.wait_ge(type_row_stored, 16 * (k + 1))
                        sp.sem_inc(type_row_kept, 1)
                    with sp.Fori(0, H) as h:
                        sp.wait_ge(head_done, b * H + h + 1)
                        for t in range(T):
                            sp.dma_start(g_rows[t], type_rows[bass.ds(h * T + t, 1), :].to_broadcast((P, N)))\
                                .then_inc(type_rows_loaded, 16)
                        with sp.Fori(0, NT) as it:
                            k = (b * H + h) * NT + it
                            sp.wait_ge(attention_done, k + 1)
                            sp.dma_start(g_adj, adj[b, bass.ds(it * P, P), :]).then_inc(adj_tile_loaded, 16)
                    for g in range(NG):
                        gg = b * NG + g
                        if g == 1:
                            sp.wait_ge(rows_final, gg)
                        sp.dma_start(xr[:, :, :], x[b, g * IW:(g + 1) * IW, :].rearrange("(t p) d -> p t d", p=P))\
                            .then_inc(rest_loaded, 16)
                        sp.wait_ge(rows_final, gg + 1)
                        sp.dma_start(out[b, g * IW:(g + 1) * IW, :].rearrange("(t p) d -> p t d", p=P),
                                     y[:, g, :, :]).then_inc(stored[g], 16)
                        sp.wait_ge(stored[g], 16 * (B + b + 1))
                    sp.sem_inc(batch_done, 1)

            second_path(sp, general)

        @block.gpsimd
        def _(pool):
            nc.gpsimd.memset(ident_b[:, :], 0.0)
            nc.gpsimd.memset(ident_f[:, :], 0.0)
            nc.gpsimd.memset(minus_half[:, :], -0.5)
            nc.gpsimd.memset(ones[:, :], 1.0)
            nc.gpsimd.memset(zeros[:, :], 0.0)
            nc.gpsimd.memset(seen[:, :], 0).then_inc(s_id, 1)
            pool.wait_ge(s_id, 1)
            for m in (ident_b, ident_f):
                last_ins = nc.gpsimd.affine_select(out=m[:, :], in_=m[:, :], compare_op=ALU.not_equal,
                                                   fill=1.0, base=0, pattern=[[-1, P]],
                                                   channel_multiplier=1)
            last_ins.then_inc(s_const, 1)
            pool.wait_ge(s_const, 1)

            def load_adj(b, g, c):
                gg = b * NG + g
                if not (known(gg) and gg == 0 and c < NCB):
                    n = gg * NCG + c - NCB
                    pool.wait_ge(adj_checked, 2 * (n + 1))
                    pool.wait_ge(mask_ready, (n + 1) * CJ)
                j0 = c * CJ * P
                nc.gpsimd.dma_start(
                    adj_b[:, c % NCB, :, :],
                    adj[b, g * IW:(g + 1) * IW, j0:j0 + CJ * P].rearrange("(t p) j -> p t j", p=P))\
                    .then_inc(adj_loaded[c % NCB], 16)

            def item_values(b, p, m):
                h, f = p * HP + m // 2, m % 2
                n = (b * NP + p) * NITEM + m
                pool.wait_ge(fac_done, b + 1)
                if not (known(n) and n == 0):
                    pool.wait_ge(lo_done, n)
                for t, w in halves:
                    nc.gpsimd.tensor_tensor(
                        v[:, t:t + w, 0:HO], he[:, he_rows(b, t, w), h * HO:(h + 1) * HO],
                        fac[:, f, t:t + w, h:h + 1].to_broadcast((P, w, HO)), ALU.mult)
                nc.gpsimd.tensor_copy(v[:, :, HO:AW], fac[:, f, :, h:h + 1]).then_inc(v_done, 1)

            def high_part(b, p, m):
                n = (b * NP + p) * NITEM + m
                h, f = p * HP + m // 2, m % 2
                pool.wait_ge(v_done, n + 1)
                if m == 0 and not (known(b) and b == 0):
                    pool.wait_ge(pv_done, (b * NG - 1) * UPG + (p + 1) * NT)
                part = (rh[:, :, h, :, 0:AW], rf[:, :, h, :, :])[f]
                nc.gpsimd.tensor_tensor(part[:, :, 0, :], v[:, :, :], ones[:, :].unsqueeze(2).to_broadcast((P, NT, AW)),
                                        ALU.mult).then_inc(hi_done, 1)

            def item(b, p, m):
                item_values(b, p, m)
                high_part(b, p, m)

            def next_group(b, g, last):
                if g + 1 < NG:
                    for c in range(NCB):
                        load_adj(b, g + 1, c)
                elif not last:
                    for c in range(NCB):
                        load_adj(b + 1, 0, c)

            for c in range(NCB):
                load_adj(0, 0, c)

            def max_of_all(b):
                pool.wait_ge(stats_done, SK * b + 1)
                nc.gpsimd.tensor_tensor(wait_pad[:, :], minus_half[:, 0:1], minus_half[:, 0:1], ALU.mult)
                nc.gpsimd.partition_all_reduce(dmax[:, :], dmax_l[:, :], P, bass.bass_isa.ReduceOp.max)\
                    .then_inc(dmax_done, 1)

            def centre(gg, g):
                pool.wait_ge(y_chain, YK * NP * (gg + 1))
                yv = y[:, g, :, :].rearrange("p t (h e) -> p (t h) e", h=H)
                nc.gpsimd.tensor_tensor(
                    yv, yv, mean1[:, :, :].rearrange("p t h -> p (t h)").unsqueeze(2).to_broadcast((P, GI * H, HO)),
                    ALU.subtract).then_inc(centred, 1)

            def normalise1_begin(gg, g):
                n = 4 * gg
                pool.wait_ge(var1_done, 2 * gg + 2)
                nc.gpsimd.tensor_tensor(rstd1[:, :], var1[:, :], minus_half[:, :], ALU.pow).then_inc(pool_chain1, 1)
                pool.wait_ge(pool_chain1, n + 1)
                yh = y[:, g, :, :].rearrange("p t (h e) -> p (t h) e", h=H)
                nc.gpsimd.tensor_tensor(yh, yh, rstd1[:, :].unsqueeze(2).to_broadcast((P, GI * H, HO)),
                                        ALU.mult).then_inc(pool_chain1, 1)

            def normalise1(gg, g):
                n = 4 * gg
                pool.wait_ge(pool_chain1, n + 2)
                yt = y[:, g, :, :]
                nc.gpsimd.tensor_tensor(yt, yt, gamma_b[:, :].unsqueeze(1).to_broadcast((P, GI, HD)),
                                        ALU.mult).then_inc(pool_chain1, 1)
                pool.wait_ge(pool_chain1, n + 3)
                nc.gpsimd.tensor_tensor(yt, yt, beta_b[:, :].unsqueeze(1).to_broadcast((P, GI, HD)),
                                        ALU.add).then_inc(pool_chain1, 1)
                pool.wait_ge(pool_chain1, n + 4)
                pool.wait_ge(xr_loaded, 16 * (gg + 1))
                nc.gpsimd.tensor_tensor(yt, yt, xr[:, :, :], ALU.add).then_inc(norm1, 1)

            def normalise2(gg, g):
                n = 3 * gg
                pool.wait_ge(var2_done, gg + 1)
                nc.gpsimd.tensor_tensor(rstd2[:, :], var2e[:, :], minus_half[:, 0:GI], ALU.pow)\
                    .then_inc(pool_chain2, 1)
                pool.wait_ge(pool_chain2, n + 1)
                nc.gpsimd.tensor_tensor(nmr2[:, :], mean2[:, g, :], rstd2[:, :], ALU.mult)\
                    .then_inc(pool_chain2, 1)
                pool.wait_ge(pool_chain2, n + 2)
                yt = y[:, g, :, :]
                nc.gpsimd.tensor_tensor(yt, yt, rstd2[:, :].unsqueeze(2).to_broadcast((P, GI, HD)), ALU.mult)\
                    .then_inc(pool_chain2, 1)
                pool.wait_ge(pool_chain2, n + 3)
                nc.gpsimd.tensor_tensor(yt, yt, nmr2[:, :].unsqueeze(2).to_broadcast((P, GI, HD)), ALU.add)\
                    .then_inc(norm2, 1)

            max_of_all(0)

            def body(b, first, last):
                for g in range(NG):
                    gg = b * NG + g
                    for c in range(NCG - NCB):
                        load_adj(b, g, c + NCB)
                        if c == 0 and not first:
                            normalise2(gg - 2, g)
                        if c == 1 and g == 0:
                            item(b, 1, 0)
                    if g == 0:
                        for m in range(1, NITEM):
                            item(b, 1, m)
                            if m == 1 and not first:
                                centre(gg - 1, 1 - g)
                    if g == 1:
                        centre(gg - 1, 1 - g)
                    next_group(b, g, last)
                    if not (first and g == 0):
                        normalise1_begin(gg - 1, 1 - g)
                    if g == NG - 1 and not last:
                        max_of_all(b + 1)
                    if not (first and g == 0):
                        normalise1(gg - 1, 1 - g)
                    if g == NG - 1 and not last:
                        for m in range(NITEM):
                            item(b + 1, 0, m)

            batches(pool, body)
            G = B * NG
            normalise2(G - 2, 0)
            pool.wait_ge(var1_done, 2 * G)
            nc.gpsimd.tensor_tensor(rstd1[:, :], var1[:, :], minus_half[:, :], ALU.pow).then_inc(last_pow, 1)
            pool.wait_ge(var2_done, G)
            nc.gpsimd.tensor_tensor(rstd2[:, :], var2e[:, :], minus_half[:, 0:GI], ALU.pow).then_inc(last_pow, 1)

            def general():
                with pool.Fori(0, B * NG) as gg:
                    pool.wait_ge(row_pow_asked, 2 * gg + 1)
                    nc.gpsimd.tensor_tensor(rstd1[:, :], var1[:, :], minus_half[:, :], ALU.pow).then_inc(row_pow, 1)
                    pool.wait_ge(row_pow_asked, 2 * gg + 2)
                    nc.gpsimd.tensor_tensor(var2[:, :], var2e[:, :], minus_half[:, 0:GI], ALU.pow)\
                        .then_inc(row_pow, 1)

            second_path(pool, general)

        @block.scalar
        def _(act):
            act.wait_ge(s_setup_pe, 1)
            nc.scalar.activation(aT, pj[0:HO, 0:ALLC], ACT.Copy)
            nc.scalar.activation(wT[:, 0:4, :], acc[0][0:HO, :].rearrange("p (k n) -> p k n", n=P), ACT.Copy)
            nc.scalar.activation(wT[:, 4:8, :], acc[1][0:HO, :].rearrange("p (k n) -> p k n", n=P), ACT.Copy)\
                .then_inc(s_setup_act, 1)
            act.wait_ge(s_setup_pe, 2)
            for c in range(DC):
                wa = acc[2][:, c * ALLC:(c + 1) * ALLC].rearrange("p (h k t) -> p k h t", h=H, k=2)
                nc.scalar.activation(w_cat[:, c, HD:PW].rearrange("p (k h) -> p k h", k=2), wa[:, :, :, 0], ACT.Copy)
                ins = nc.scalar.activation(w_all[:, c, :].rearrange("p (k h t) -> p k h t", k=2, h=H), wa, ACT.Copy)
            ins.then_inc(s_setup_act, 1)

            def copy_xT(b, q):
                k = b * HALF + q
                act.wait_ge(tx_done, k + 1)
                if not (known(k) and k == 0):
                    act.wait_ge(mm_done, 2 * k)
                nc.scalar.activation(xT[:, :, :, :], pj[:, :].rearrange("p (a c n) -> p a c n", a=2, c=DC),
                                     ACT.Copy).then_inc(xt_copied, 1)

            def copy_he(b, n, i):
                k = b * HALF + n
                slots = he_rows(b, 2 * PAIR_ORDER[n] + i)
                act.wait_ge(mm_done, 2 * k + i + 1)
                if n == HALF // 2 and i == 0 and not (known(b) and b == 0):
                    act.wait_ge(y_chain, YK * ((b - 1) * NG * NP + 1) + 8)
                bank = first_banks(n, i) if known(b) and b == 0 else pj
                nc.scalar.activation(he[:, slots, :], bank[:, 0:PW].unsqueeze(1), ACT.Copy)\
                    .then_inc(he_copied, 1)

            def factors(b):
                act.wait_ge(pro_done, b + 1)
                nc.scalar.activation(fac[:, 0, :, :], d_sh[:, :, :], ACT.Exp)
                nc.scalar.activation(fac[:, 1, :, :], d_sh[:, :, :], ACT.Exp, scale=SLOPE)
                nc.scalar.activation(g_fac[:, bass.ds(b % 2, 1), :, :].rearrange("p o t h -> p (o t) h"),
                                     sg_sh[:, :, :], ACT.Exp, scale=SLOPE - 1.0).then_inc(exps_done, 1)

            def rows(b):
                act.wait_ge(st_pe, b + 1)
                if not (known(b) and b == 0):
                    act.wait_ge(rows_stored, 16 * b)
                nc.scalar.activation(sT[:, :], pj[:, 0:P], ACT.Copy).then_inc(st_act, 1)

            def positive(b, g, p, u, k):
                uu = (b * NG + g) * UPG + p * NT + u
                if u == 0 and k == 0:
                    act.wait_ge(s_loaded[p], 16 * (b * NG + g + 1))
                    act.wait_ge(pro_done, b + 1)
                if k == 0 and not (known(uu) and uu < 2):
                    act.wait_ge(b_ready, uu - 1)
                col = u * H + p * HP + k
                bias_ap = d_big[:, bass.ds(b % 2, 1), col:col + 1].rearrange("p o c -> p (o c)")
                nc.scalar.activation(r[:, u % 2, k, :], s_bc[:, p, k, :], ACT.Relu, bias=bias_ap, scale=BIG)\
                    .then_inc(r_ready, 1)

            def square1(gg, g, part, parts):
                if part == 0:
                    act.wait_ge(centred, gg + 1)
                    if not (known(gg) and gg == 0):
                        act.wait_ge(squared2, gg)
                t, w = part * GI // parts, GI // parts
                ins = nc.scalar.activation(o_flat[:, t * HD:(t + w) * HD].rearrange("p (t e) -> p t e", e=HO),
                                           y[:, g, t:t + w, :].rearrange("p t (h e) -> p (t h) e", h=H),
                                           ACT.Square)
                if part == parts - 1:
                    ins.then_inc(squared1, 1)

            o_flat = o[:, :, :].rearrange("p n w -> p (n w)")[:, 0:GI * HD]

            def square2(gg, g, steps, part, parts):
                if part == 0:
                    act.wait_ge(sum2_done, 2 * gg + 2)
                    act.wait_ge(y_chain, steps)
                    if not (known(gg) and gg == 0):
                        act.wait_ge(var2_done, gg)
                for it in range(part * GI // parts, (part + 1) * GI // parts):
                    ins = nc.scalar.activation(o_flat[:, it * HD:(it + 1) * HD], y[:, g, it, :], ACT.Square,
                                               bias=mean2[:, g, it:it + 1], accum_out=var2[:, it:it + 1])
                if part == parts - 1:
                    ins.then_inc(squared2, 1)

            def acc_out(b, g, p):
                pp = (b * NG + g) * NP + p
                if p == 0:
                    if not (known(pp) and pp == 0):
                        act.wait_ge(var1_done, 2 * (b * NG + g))
                        act.wait_ge(y_chain, YK * pp)
                else:
                    act.wait_ge(y_chain, YK * pp)
                for k in ACT_BANKS:
                    a, e = bank_pairs(k)
                    act.wait_ge(bank_done, (NAB - 1) * pp + k + 1)
                    nc.scalar.activation(o[:, a:e, :].rearrange("p n w -> p (n w)"),
                                         acc[k][:, 0:(e - a) * 2 * AW], ACT.Copy).then_inc(acc_out_act, 1)

            copy_xT(0, 0)
            for q in range(HALF):
                copy_he(0, q, 0)
                if q + 1 < HALF:
                    copy_xT(0, q + 1)
                copy_he(0, q, 1)
            factors(0)
            rows(0)
            for m in range(NITEM):
                act.wait_ge(v_done, m + 1)
                part = (rh[:, :, m // 2, :, 0:AW], rf[:, :, m // 2, :, :])[m % 2]
                nc.scalar.activation(part[:, :, 0, :], v[:, :, :], ACT.Copy).then_inc(hi_done, 1)

            def body(b, first, last):
                for g in range(NG):
                    gg = b * NG + g
                    for p in range(NP):
                        for u in range(NT):
                            for k in range(HP):
                                if u > 0 or (first and g == 0 and p == 0):
                                    positive(b, g, p, u, k)
                            if not last and projection_step(g, p, u, 1):
                                q, step = projection_step(g, p, u, 1)
                                if step == 0:
                                    copy_xT(b + 1, q)
                                else:
                                    copy_he(b + 1, q, step - 1)
                            if p == 0 and u >= NT - 4 and not (first and g == 0):
                                square1(gg - 1, 1 - g, u - (NT - 4), 4)
                            if p == 1 and 11 <= u < 15 and not (first and g == 0):
                                square2(gg - 1, 1 - g, YK * (gg * NP + 1), u - 11, 4)
                            if g == 1 and p == 1 and not last:
                                if u == 5:
                                    rows(b + 1)
                                    factors(b + 1)
                        if not (last and g == NG - 1 and p == NP - 1):
                            for k in range(HP):
                                positive(*((b, g, 1) if p == 0 else (b, 1, 0) if g == 0 else (b + 1, 0, 0)), 0, k)
                        acc_out(b, g, p)

            batches(act, body)
            G = B * NG
            square1(G - 1, 1, 0, 1)
            square2(G - 1, 1, YK * G * NP, 0, 1)

            def general():
                with act.Fori(0, B) as b:
                    with act.Fori(0, NT) as t:
                        k = b * NT + t
                        act.wait_ge(x_tile_transposed, k + 1)
                        nc.scalar.activation(xT[:, 0, :, :], pj[:, 0:D].rearrange("p (c n) -> p c n", c=DC), ACT.Copy)\
                            .then_inc(x_tile_copied, 1)
                        act.wait_ge(tile_products, k + 1)
                        nc.scalar.activation(he[:, bass.ds(t, 1), 0:HD], pj[:, 0:HD].unsqueeze(1), ACT.Copy)
                        nc.scalar.activation(g_src[:, bass.ds(t, 1), :], acc[0][:, 0:H * T].unsqueeze(1), ACT.Copy)
                        nc.scalar.activation(g_dst_row, acc[1][0:H * T, 0:P], ACT.Copy).then_inc(tile_projected, 1)
                    with act.Fori(0, H * NT) as n:
                        k = b * (H * NT) + n
                        act.wait_ge(weight_steps, WS * (k + 1))
                        nc.scalar.activation(g_w, g_w, ACT.Exp, bias=g_max, accum_out=g_sum).then_inc(exp_done, 1)
                        act.wait_ge(exp_transposed, k + 1)
                        for q in range(NT // 4):
                            ins = nc.scalar.activation(g_expT[:, 4 * q:4 * q + 4, :],
                                                       acc[q][:, :].rearrange("p (t n) -> p t n", t=4), ACT.Copy)
                        ins.then_inc(exp_copied, 1)

            second_path(act, general)

        @block.vector
        def _(dve):
            nc.vector.memset(eabs[:, :], 0.0)
            nc.vector.memset(dlow[:, :], 0.0)
            nc.vector.memset(habs[:, :], 0.0)
            nc.vector.memset(dmin[:, :], 1.0).then_inc(s_memset, 1)

            def stats(b):
                dve.wait_ge(he_copied, NT * (b + 1))
                if not (known(b) and b == 0):
                    dve.wait_ge(dmax_done, b)
                    dve.wait_ge(st_pe, b)
                for t, m in halves:
                    rows_ = he[:, he_rows(b, t, m), :]
                    nc.vector.tensor_copy(s_hn[:, 0, :].rearrange("p (h t) -> p t h", h=H)[:, t:t + m, :],
                                          rows_[:, :, HD:HD + H])
                    ins = nc.vector.tensor_copy(s_hn[:, 1, :].rearrange("p (h t) -> p t h", h=H)[:, t:t + m, :],
                                                rows_[:, :, HD + H:PW])
                ins.then_inc(st_vec, 1)
                dve.wait_ge(st_vec, b + 1)
                nc.vector.tensor_reduce(dmax_l[:, :], s_hn[:, 1, :].rearrange("p (h t) -> p h t", h=H), AX.X, ALU.max)\
                    .then_inc(stats_done, 1)
                nc.vector.tensor_reduce(eabs[:, 1:2], s_hn[:, :, :].rearrange("p k n -> p (k n)"), AX.X, ALU.max,
                                        apply_absolute_value=True).then_inc(stats_done, 1)

            def shifts(b):
                dve.wait_ge(stats_done, SK * b + 2)
                nc.vector.tensor_tensor(eabs[:, 0:1], eabs[:, 0:1], eabs[:, 1:2], ALU.max)
                nc.vector.tensor_scalar(d_big[:, bass.ds(b % 2, 1), :].rearrange("p o (t h) -> p (o h) t", h=H),
                                        s_hn[:, 1, :].rearrange("p (h t) -> p h t", h=H), BIG, None, ALU.mult)
                dve.wait_ge(dmax_done, b + 1)
                if not (known(b) and b == 0):
                    dve.wait_ge(exps_done, b)
                gmax = dmax[:, :].unsqueeze(1).to_broadcast((P, NT, H))
                nc.vector.tensor_tensor(sg_sh[:, :, :], s_hn[:, 0, :].rearrange("p (h t) -> p t h", h=H), gmax, ALU.add)\
                    .then_inc(sums_done, 1)
                dve.wait_ge(sums_done, b + 1)
                nc.vector.tensor_scalar(sg_sh[:, :, :], sg_sh[:, :, :], -3 * MAX_SCORE, None, ALU.max)
                nc.vector.tensor_tensor(d_sh[:, :, :], s_hn[:, 1, :].rearrange("p (h t) -> p t h", h=H), gmax,
                                        ALU.subtract).then_inc(pro_done, 1)
                dve.wait_ge(pro_done, b + 1)
                nc.vector.tensor_reduce(dlow[:, 1:2], d_sh[:, :, :].rearrange("p t h -> p (t h)"), AX.X, ALU.min)\
                    .then_inc(spread_seen, 1)
                dve.wait_ge(spread_seen, b + 1)
                nc.vector.tensor_tensor(dlow[:, 0:1], dlow[:, 0:1], dlow[:, 1:2], ALU.min)

            def check_values(b, half, h):
                t, w = halves[half]
                if h == 0 and half == 1:
                    dve.wait_ge(he_copied, NT * b + HALF)
                    if not (known(b) and b == 0):
                        dve.wait_ge(fac_done, b)
                if h == 0 and half == 0:
                    dve.wait_ge(he_copied, NT * (b + 1))
                ins = nc.vector.tensor_reduce(habs_part[:, half, h:h + 1],
                                              he[:, he_rows(b, t, w), h * HO:(h + 1) * HO], AX.XY, ALU.max,
                                              apply_absolute_value=True)
                if h == H - 1 and half == 0:
                    ins.then_inc(values_seen, 1)

            def scale_factors(b):
                dve.wait_ge(values_seen, 3 * b + 1)
                nc.vector.tensor_reduce(hmax[:, :], habs_part[:, :, :].rearrange("p a h -> p (a h)"), AX.X, ALU.max)\
                    .then_inc(values_seen, 1)
                dve.wait_ge(values_seen, 3 * b + 2)
                nc.vector.tensor_tensor(habs[:, :], habs[:, :], hmax[:, :], ALU.max)
                nc.vector.tensor_scalar(fits[:, :], hmax[:, :], MAX_VALUE, SCALE, ALU.is_le, ALU.mult)\
                    .then_inc(values_seen, 1)
                dve.wait_ge(values_seen, 3 * b + 3)
                dve.wait_ge(exps_done, b + 1)
                ff = fac[:, :, :, :].rearrange("p f t h -> p (f t h)")
                nc.vector.tensor_scalar(ff, ff, fits[:, :], None, ALU.mult).then_inc(fac_done, 1)

            def negate(b, p):
                dve.wait_ge(lo_done, (b * NP + p + 1) * NITEM)
                for k in range(HP):
                    h = p * HP + k
                    for part in range(2):
                        ins = nc.vector.tensor_scalar(rh[:, :, h, part, AW:2 * AW], rf[:, :, h, part, :], -1.0, None,
                                                      ALU.mult)
                ins.then_inc(neg_done, 1)

            def copy_mask(b, g, u):
                jj = (b * NG + g) * NT + u
                dve.wait_ge(mask_ready, jj + 1)
                if not (known(b, g) and b == 0 and g == 0):
                    dve.wait_ge(pv_done, (b * NG + g - 1) * UPG + NT + u + 1)
                nc.vector.tensor_copy(mask[:, u, :], mT[:, :]).then_inc(mask_copied, 1)

            def not_positive(b, g, p, u):
                dve.wait_ge(b_ready, (b * NG + g) * UPG + p * NT + u + 1)
                nc.vector.tensor_tensor(b_neg[:, u % 2, :], mask[:, u, :], b_pos[:, u % 2, 0, :], ALU.subtract)\
                    .then_inc(neg_ready, 1)

            def probs(b, g, p, u):
                uu = (b * NG + g) * UPG + p * NT + u
                if p == 0:
                    dve.wait_ge(mask_copied, (b * NG + g) * NT + u + 1)
                dve.wait_ge(r_ready, HP * (uu + 1))
                if not (known(uu) and uu < 2):
                    dve.wait_ge(pv_done, uu - 1)
                nc.vector.tensor_tensor(b_pos[:, u % 2, :, :], r[:, u % 2, :, :],
                                        mask[:, u, :].unsqueeze(1).to_broadcast((P, HP, IW)), ALU.min)\
                    .then_inc(b_ready, 1)

            def check_adj(b, g, c):
                n = (b * NG + g) * NCG + c
                dve.wait_ge(adj_loaded[c % NCB], 16 * ((b * NG + g) * (NCG // NCB) + c // NCB + 1))
                bits = adj_b[:, c % NCB, :, :].rearrange("p t j -> p (t j)").bitcast(I32)
                w = GI * CJ * P // 4
                for i in range(2):
                    if not (known(n) and n == 0 and i == 0):
                        dve.wait_ge(adj_checked, 2 * n + i)
                    nc.vector.tensor_tensor(seen[:, :], seen[:, :], bits[:, i * w:(i + 1) * w],
                                            ALU.bitwise_or).then_inc(adj_checked, 1)

            def item_low(b, p, m):
                h, f = p * HP + m // 2, m % 2
                dve.wait_ge(hi_done, (b * NP + p) * NITEM + m + 1)
                part = (rh[:, :, h, :, 0:AW], rf[:, :, h, :, :])[f]
                nc.vector.tensor_tensor(part[:, :, 1, :], v[:, :, :], part[:, :, 0, :], ALU.subtract)\
                    .then_inc(lo_done, 1)

            def build(b, p, u):
                if u in LOW_AT[p]:
                    item_low(b, p, LOW_AT[p].index(u))
                if u == LOW_AT[p][-1]:
                    negate(b, p)

            def acc_out(b, g, p):
                pp = (b * NG + g) * NP + p
                gg = b * NG + g
                if not (known(pp) and pp <= 1):
                    if p == 0:
                        dve.wait_ge(var1_done, 2 * gg)
                    else:
                        dve.wait_ge(squared2, gg)
                for k in DVE_BANKS:
                    a, e = bank_pairs(k)
                    if k < NAB - 1:
                        dve.wait_ge(bank_done, (NAB - 1) * pp + k + 1)
                    else:
                        dve.wait_ge(pv_done, (pp + 1) * NT)
                    nc.vector.tensor_copy(o[:, a:e, :].rearrange("p n w -> p (n w)"),
                                          acc[k][:, 0:(e - a) * 2 * AW]).then_inc(acc_out_dve, 1)

            def finish(b, g, p, step):
                pp = (b * NG + g) * NP + p
                gg = b * NG + g
                n = YK * pp
                cols = slice(p * HP * HO, (p + 1) * HP * HO)
                yt = y[:, g, :, cols]
                yh = yt.rearrange("p t (h e) -> p t h e", h=HP)
                oh = o[:, :, :].rearrange("p (t h) w -> p t h w", h=HP)
                den = o[:, :, HO:AW].rearrange("p n o -> p (n o)")
                m1 = mean1[:, :, p * HP:(p + 1) * HP]
                if step == 0:
                    dve.wait_ge(acc_out_dve, len(DVE_BANKS) * (pp + 1))
                    dve.wait_ge(acc_out_act, len(ACT_BANKS) * (pp + 1))
                    gsc = g_fac[:, bass.ds(b % 2, 1), g * GI:(g + 1) * GI, p * HP:(p + 1) * HP]\
                        .rearrange("p o t h -> p (o t) h").unsqueeze(3).to_broadcast((P, GI, HP, AW))
                    nc.vector.tensor_tensor(oh[:, :, :, AW:2 * AW], oh[:, :, :, AW:2 * AW], gsc, ALU.mult)\
                        .then_inc(y_chain, 1)
                if step == 1:
                    dve.wait_ge(y_chain, n + 1)
                    nc.vector.tensor_tensor(o[:, :, 0:AW], o[:, :, 0:AW], o[:, :, AW:2 * AW], ALU.add)\
                        .then_inc(y_chain, 1)
                if step == 2:
                    dve.wait_ge(y_chain, n + 2)
                    nc.vector.tensor_reduce(dmin[:, 1:2], den, AX.X, ALU.min).then_inc(y_chain, 1)
                    nc.vector.tensor_scalar(rden[:, :], den, TINY, None, ALU.max).then_inc(y_chain, 1)
                if step == 3:
                    dve.wait_ge(y_chain, n + 4)
                    nc.vector.reciprocal(rden[:, :], rden[:, :]).then_inc(y_chain, 1)
                    nc.vector.tensor_tensor(dmin[:, 0:1], dmin[:, 0:1], dmin[:, 1:2], ALU.min)
                    if p == 0 and not (known(gg) and gg < NG):
                        dve.wait_ge(stored[g], 16 * b)
                    dve.wait_ge(y_chain, n + 5)
                    nc.vector.tensor_tensor(yh, oh[:, :, :, 0:HO],
                                            rden[:, :].rearrange("p (t h) -> p t h", h=HP).unsqueeze(3)
                                            .to_broadcast((P, GI, HP, HO)), ALU.mult).then_inc(y_chain, 1)
                if step == 4:
                    dve.wait_ge(y_chain, n + 6)
                    nc.vector.tensor_tensor(yt, yt, bias_b[:, cols].unsqueeze(1).to_broadcast((P, GI, HP * HO)),
                                            ALU.add).then_inc(y_chain, 1)
                if step == 5:
                    dve.wait_ge(y_chain, n + 7)
                    nc.vector.scalar_tensor_tensor(yt, yt, 0.0, he[:, he_rows(b, g * GI, GI), cols],
                                                   ALU.max, ALU.add).then_inc(y_chain, 1)
                if step == 6:
                    dve.wait_ge(y_chain, n + 8)
                    if p == 0 and not (known(gg) and gg == 0):
                        dve.wait_ge(centred, gg)
                    nc.vector.tensor_reduce(m1, yh, AX.X, ALU.add).then_inc(y_chain, 1)
                if step == 7:
                    dve.wait_ge(y_chain, n + 9)
                    nc.vector.tensor_scalar(m1, m1, 1.0 / HO, None, ALU.mult).then_inc(y_chain, 1)

            def variance1(gg):
                dve.wait_ge(squared1, gg + 1)
                if not (known(gg) and gg == 0):
                    dve.wait_ge(norm1, gg)
                nc.vector.tensor_reduce(var1[:, :], o[:, :, :].rearrange("p n w -> p (n w)")[:, 0:GI * HD]
                                        .rearrange("p (t e) -> p t e", e=HO), AX.X, ALU.add).then_inc(var1_done, 1)
                dve.wait_ge(var1_done, 2 * gg + 1)
                nc.vector.tensor_scalar(var1[:, :], var1[:, :], 1.0 / HO, LN1_EPS, ALU.mult, ALU.add)\
                    .then_inc(var1_done, 1)

            def sum2(gg, g):
                dve.wait_ge(norm1, gg + 1)
                nc.vector.tensor_reduce(mean2[:, g, :], y[:, g, :, :], AX.X, ALU.add).then_inc(sum2_done, 1)
                dve.wait_ge(sum2_done, 2 * gg + 1)
                nc.vector.tensor_scalar(mean2[:, g, :], mean2[:, g, :], -1.0 / HD, None, ALU.mult)\
                    .then_inc(sum2_done, 1)

            def variance2(gg):
                dve.wait_ge(squared2, gg + 1)
                if not (known(gg) and gg == 0):
                    dve.wait_ge(norm2, gg)
                nc.vector.tensor_scalar(var2e[:, :], var2[:, :], 1.0 / HD, LN2_EPS, ALU.mult, ALU.add)\
                    .then_inc(var2_done, 1)

            dve.wait_ge(s_memset, 1)
            dve.wait_ge(s_id, 1)
            dve.wait_ge(s_vec, 48)
            for h in range(H):
                check_values(0, 1, h)
            stats(0)
            shifts(0)
            for h in range(H):
                check_values(0, 0, h)
            scale_factors(0)
            for m in range(NITEM):
                h, f = m // 2, m % 2
                dve.wait_ge(fac_done, 1)
                if m > 0:
                    dve.wait_ge(lo_done, m)
                for t, w in halves:
                    nc.vector.tensor_tensor(
                        v[:, t:t + w, 0:HO], he[:, he_rows(0, t, w), h * HO:(h + 1) * HO],
                        fac[:, f, t:t + w, h:h + 1].to_broadcast((P, w, HO)), ALU.mult)
                nc.vector.tensor_copy(v[:, :, HO:AW], fac[:, f, :, h:h + 1]).then_inc(v_done, 1)
                item_low(0, 0, m)
            negate(0, 0)

            def body(b, first, last):
                for g in range(NG):
                    gg = b * NG + g
                    for p in range(NP):
                        pp = gg * NP + p
                        before = (b, g, 0) if p else (b, 0, 1) if g else (b - 1, 1, 1)
                        if first and g == 0 and p == 0:
                            before = None
                            copy_mask(b, g, 0)
                            copy_mask(b, g, 1)
                        for u in range(NT):
                            probs(b, g, p, u)
                            if apart(g, p):
                                not_positive(b, g, p, u)
                            if u == 0 and before:
                                acc_out(*before)
                            elif before and u <= 8:
                                finish(*before, u - 1)
                            if p == 0:
                                if u + 2 < NT:
                                    copy_mask(b, g, u + 2)
                                if u % CJ == CJ - 1:
                                    check_adj(b, g, u // CJ)
                                if u == 15 and before:
                                    variance1(gg - 1)
                            else:
                                if u == 10 and not (first and g == 0):
                                    sum2(gg - 1, 1 - g)
                                if u >= NT - 2 and not (last and g == NG - 1):
                                    copy_mask(*((b, g + 1) if g + 1 < NG else (b + 1, 0)), u + 2 - NT)
                                if u == 15 and not (first and g == 0):
                                    variance2(gg - 1)
                            if g == 0 and p == 0:
                                build(b, 1, u)
                            if g == 1 and p == 0 and not last and 9 <= u < 9 + H:
                                check_values(b + 1, 1, u - 9)
                            if g == 1 and p == 1 and not last:
                                if u == 2:
                                    stats(b + 1)
                                if 3 <= u < 3 + H:
                                    check_values(b + 1, 0, u - 3)
                                if u == 4:
                                    shifts(b + 1)
                                if u == 6:
                                    scale_factors(b + 1)
                                build(b + 1, 0, u)

            batches(dve, body)
            G = B * NG
            acc_out(B - 1, 1, 1)
            for step in range(8):
                finish(B - 1, 1, 1, step)
            yt = y[:, NG - 1, :, :]
            yh = yt.rearrange("p t (h e) -> p (t h) e", h=H)
            dve.wait_ge(y_chain, YK * NP * G)
            nc.vector.tensor_tensor(yh, yh, mean1[:, :, :].rearrange("p t h -> p (t h)").unsqueeze(2)
                                    .to_broadcast((P, GI * H, HO)), ALU.subtract).then_inc(centred, 1)
            variance1(G - 1)
            dve.wait_ge(last_pow, 1)
            nc.vector.tensor_tensor(yh, yh, rstd1[:, :].unsqueeze(2).to_broadcast((P, GI * H, HO)),
                                    ALU.mult).then_inc(last_steps, 1)
            dve.wait_ge(last_steps, 1)
            nc.vector.tensor_tensor(yt, yt, gamma_b[:, :].unsqueeze(1).to_broadcast((P, GI, HD)),
                                    ALU.mult).then_inc(last_steps, 1)
            dve.wait_ge(last_steps, 2)
            nc.vector.tensor_tensor(yt, yt, beta_b[:, :].unsqueeze(1).to_broadcast((P, GI, HD)),
                                    ALU.add).then_inc(last_steps, 1)
            dve.wait_ge(last_steps, 3)
            dve.wait_ge(xr_loaded, 16 * G)
            nc.vector.tensor_tensor(yt, yt, xr[:, :, :], ALU.add).then_inc(norm1, 1)
            sum2(G - 1, 1)
            variance2(G - 1)
            dve.wait_ge(last_pow, 2)
            nc.vector.tensor_tensor(nmr2[:, :], mean2[:, NG - 1, :], rstd2[:, :], ALU.mult)
            nc.vector.tensor_tensor(yt, yt, rstd2[:, :].unsqueeze(2).to_broadcast((P, GI, HD)), ALU.mult)\
                .then_inc(last_steps, 1)
            dve.wait_ge(last_steps, 4)
            nc.vector.tensor_tensor(yt, yt, nmr2[:, :].unsqueeze(2).to_broadcast((P, GI, HD)), ALU.add)\
                .then_inc(norm2, 1)

            seen_bits = seen[:, 0:GI * CJ * P // 4]
            nc.vector.tensor_scalar(seen_bits, seen_bits, ~ONES, None, ALU.bitwise_and).then_inc(tested, 1)
            dve.wait_ge(tested, 1)
            nc.vector.tensor_scalar(seen_any, seen_bits, 0, None, ALU.not_equal).then_inc(tested, 1)
            dve.wait_ge(tested, 2)
            nc.vector.tensor_reduce(tests[:, 0:1], seen_any, AX.X, ALU.max)
            nc.vector.tensor_scalar(tests[:, 1:2], eabs[:, 0:1], MAX_SCORE, None, ALU.is_gt)
            nc.vector.tensor_scalar(tests[:, 2:3], dlow[:, 0:1], -MAX_SPREAD, None, ALU.is_lt)
            nc.vector.tensor_scalar(tests[:, 3:4], habs[:, :], MAX_VALUE, None, ALU.is_gt)
            nc.vector.tensor_scalar(tests[:, 4:5], dmin[:, 0:1], 0.0, None, ALU.is_le).then_inc(tested, 1)
            dve.wait_ge(tested, 3)
            nc.vector.tensor_reduce(beyond[:, :], tests[:, :], AX.X, ALU.max).then_inc(tested, 1)
            dve.wait_ge(beyond_summed, 1)
            for i, free in enumerate((tile_projected, head_done, attention_done, batch_done)):
                nc.vector.memset(step_pad[:, i:i + 1], 0.0).then_inc(free, 1)
            nc.vector.tensor_copy(flag[:, :], pj[0:1, 0:1]).then_inc(flag_ready, 1)

            def weights_of_tile(b, h, it):
                k = (b * H + h) * NT + it
                n = WS * k
                dve.wait_ge(type_rows_loaded, 16 * T * (b * H + h + 1))
                dve.wait_ge(adj_tile_loaded, 16 * (k + 1))
                nc.vector.tensor_copy(g_s, g_src[:, bass.ds(it, 1), :]
                                      .rearrange("p o (h t) -> p (o h) t", h=H)[:, bass.ds(h, 1), :]
                                      .rearrange("p o t -> p (o t)")).then_inc(weight_steps, 1)
                dve.wait_ge(weight_steps, n + 1)
                n += 1
                for t in range(T):
                    dst = g_w if t == 0 else g_part
                    nc.vector.tensor_scalar(dst, g_rows[t], g_s[:, t:t + 1], None, ALU.add).then_inc(weight_steps, 1)
                    dve.wait_ge(weight_steps, n + 1)
                    nc.vector.scalar_tensor_tensor(dst, g_adj, float(t + 1), dst, ALU.is_equal, ALU.mult)\
                        .then_inc(weight_steps, 1)
                    dve.wait_ge(weight_steps, n + 2)
                    n += 2
                    if t > 0:
                        nc.vector.tensor_tensor(g_w, g_w, g_part, ALU.add).then_inc(weight_steps, 1)
                        dve.wait_ge(weight_steps, n + 1)
                        n += 1
                nc.vector.scalar_tensor_tensor(g_w, g_w, SLOPE, g_w, ALU.mult, ALU.max)
                nc.vector.tensor_scalar(g_part, g_adj, 0.0, NEG, ALU.is_equal, ALU.mult).then_inc(weight_steps, 1)
                dve.wait_ge(weight_steps, n + 1)
                nc.vector.tensor_tensor(g_w, g_w, g_part, ALU.add).then_inc(weight_steps, 1)
                dve.wait_ge(weight_steps, n + 2)
                nc.vector.tensor_reduce(g_inv, g_w, AX.X, ALU.max).then_inc(weight_steps, 1)
                dve.wait_ge(weight_steps, n + 3)
                nc.vector.tensor_scalar(g_max, g_inv, -1.0, None, ALU.mult).then_inc(weight_steps, 1)

            def finish_rows(b, g):
                gg = b * NG + g
                n = [RS * gg]
                yt = y[:, g, :, :]
                yh = yt.rearrange("p t (h e) -> p (t h) e", h=H)
                sq = g_tmp.rearrange("p (t e) -> p t e", e=HO)[:, 0:GI * H, :]
                m1 = mean1[:, :, :].rearrange("p t h -> p (t h)")

                def done(ins):
                    ins.then_inc(row_steps, 1)
                    n[0] += 1
                    dve.wait_ge(row_steps, n[0])

                def wide(a, w):
                    return a.unsqueeze(2).to_broadcast((P, a.shape[1], w))

                vec = nc.vector
                done(vec.tensor_tensor(yt, yt, bias_b[:, :].unsqueeze(1).to_broadcast((P, GI, HD)), ALU.add))
                done(vec.scalar_tensor_tensor(yt, yt, 0.0, he[:, g * GI:(g + 1) * GI, 0:HD], ALU.max, ALU.add))
                done(vec.tensor_reduce(m1, yh, AX.X, ALU.add))
                done(vec.tensor_scalar(m1, m1, 1.0 / HO, None, ALU.mult))
                done(vec.tensor_tensor(yh, yh, wide(m1, HO), ALU.subtract))
                done(vec.tensor_tensor(sq, yh, yh, ALU.mult))
                done(vec.tensor_reduce(var1[:, :], sq, AX.X, ALU.add))
                vec.tensor_scalar(var1[:, :], var1[:, :], 1.0 / HO, LN1_EPS, ALU.mult, ALU.add)\
                    .then_inc(row_pow_asked, 1)
                dve.wait_ge(row_pow, 2 * gg + 1)
                done(vec.tensor_tensor(yh, yh, wide(rstd1[:, :], HO), ALU.mult))
                done(vec.tensor_tensor(yt, yt, gamma_b[:, :].unsqueeze(1).to_broadcast((P, GI, HD)), ALU.mult))
                done(vec.tensor_tensor(yt, yt, beta_b[:, :].unsqueeze(1).to_broadcast((P, GI, HD)), ALU.add))
                dve.wait_ge(rest_loaded, 16 * (gg + 1))
                done(vec.tensor_tensor(yt, yt, xr[:, :, :], ALU.add))
                m2 = mean2[:, g, :]
                done(vec.tensor_reduce(m2, yt, AX.X, ALU.add))
                done(vec.tensor_scalar(m2, m2, 1.0 / HD, None, ALU.mult))
                done(vec.tensor_tensor(yt, yt, wide(m2, HD), ALU.subtract))
                sq2 = g_tmp.rearrange("p (t e) -> p t e", e=HD)[:, 0:GI, :]
                done(vec.tensor_tensor(sq2, yt, yt, ALU.mult))
                done(vec.tensor_reduce(var2e[:, :], sq2, AX.X, ALU.add))
                vec.tensor_scalar(var2e[:, :], var2e[:, :], 1.0 / HD, LN2_EPS, ALU.mult, ALU.add)\
                    .then_inc(row_pow_asked, 1)
                dve.wait_ge(row_pow, 2 * gg + 2)
                done(vec.tensor_tensor(yt, yt, wide(var2[:, :], HD), ALU.mult))
                vec.memset(step_pad[:, 5:6], 0.0).then_inc(rows_final, 1)

            def general():
                with dve.Fori(0, B) as b:
                    with dve.Fori(0, H) as h:
                        hh = b * H + h
                        dve.wait_ge(tile_projected, (b + 1) * NT + 1)
                        nc.vector.tensor_copy(
                            g_head.unsqueeze(2), he[:, 0:NT, 0:HD].rearrange("p t (h e) -> p t h e", h=H)
                            [:, :, bass.ds(h, 1), :]).then_inc(head_copied, 1)
                        with dve.Fori(0, NT) as it:
                            k = hh * NT + it
                            weights_of_tile(b, h, it)
                            dve.wait_ge(exp_done, k + 1)
                            nc.vector.reciprocal(g_inv, g_sum).then_inc(inverse_done, 1)
                            dve.wait_ge(inverse_done, k + 1)
                            dve.wait_ge(attention_product, k + 1)
                            nc.vector.tensor_scalar(
                                g_y.rearrange("p t (h e) -> p t h e", h=H)[:, bass.ds(it, 1), :, :]
                                .rearrange("p o h e -> p (o h) e")[:, bass.ds(h, 1), :]
                                .rearrange("p o e -> p (o e)"),
                                acc[4][:, 0:HO], g_inv, None, ALU.mult).then_inc(attention_done, 1)
                        nc.vector.memset(step_pad[:, 4:5], 0.0).then_inc(head_done, 1)
                    for g in range(NG):
                        finish_rows(b, g)

            second_path(dve, general)

        @block.tensor
        def _(pe):
            pe.wait_ge(s_const, 1)
            pe.wait_ge(s_w, 16 * (DC + 2))
            nc.tensor.transpose(pj[0:HO, 0:ALLC], a_rows, ident_f[0:ALLC, 0:ALLC])
            for c in range(DC):
                for h in range(H):
                    k = c * H + h
                    ins = nc.tensor.transpose(acc[k // 4][0:HO, (k % 4) * P:(k % 4 + 1) * P],
                                              w_cat[:, c, h * HO:(h + 1) * HO], ident_f[:, :])
            ins.then_inc(s_setup_pe, 1)
            pe.wait_ge(s_setup_act, 1)
            for c in range(DC):
                for h in range(H):
                    k = c * H + h
                    ins = nc.tensor.matmul(
                        acc[2][:, k * 2 * T:(k + 1) * 2 * T].rearrange("p (k t) -> p k t", k=2), wT[:, k, :],
                        aT.rearrange("p (k h t) -> p k h t", k=2, h=H)[:, :, h, :],
                        start=(k == 0), stop=True, skip_group_check=True)
            ins.then_inc(s_setup_pe, 1)

            def transpose_x(b, q):
                k = b * HALF + q
                pe.wait_ge(xp_loaded, 16 * (k + 1))
                if known(b) and b == 0:
                    if q > 0:
                        pe.wait_ge(xt_copied, q)
                else:
                    pe.wait_ge(he_copied, 2 * k)
                for i in range(2):
                    for c in range(DC):
                        ins = nc.tensor.transpose(pj[:, (i * DC + c) * P:(i * DC + c + 1) * P],
                                                  x_pair[:, i, c * P:(c + 1) * P], ident_f[:, :])
                ins.then_inc(tx_done, 1)

            def project(b, q, i):
                k = b * HALF + q
                bank = pj
                if i == 0:
                    pe.wait_ge(xt_copied, k + 1)
                if known(b) and b == 0:
                    bank = first_banks(q, i)
                    if q >= 2:
                        pe.wait_ge(he_copied, 2 * q - 3 + i)
                elif i == 1:
                    pe.wait_ge(he_copied, 2 * k + 1)
                for c in range(DC):
                    ins = nc.tensor.matmul(bank[:, 0:PW], xT[:, i, c, :], w_cat[:, c, :],
                                           start=(c == 0), stop=(c == DC - 1))
                ins.then_inc(mm_done, 1)

            def score_row(b):
                pe.wait_ge(st_vec, b + 1)
                pe.wait_ge(he_copied, NT * (b + 1))
                nc.tensor.transpose(pj[:, 0:P], s_hn[:, :, :].rearrange("p k n -> p (k n)"), ident_f[:, :])\
                    .then_inc(st_pe, 1)

            def transpose_mask(b, g, u):
                c = u // CJ
                jj = (b * NG + g) * NT + u
                if u % CJ == 0:
                    pe.wait_ge(adj_loaded[c % NCB], 16 * ((b * NG + g) * (NCG // NCB) + c // NCB + 1))
                if not (known(jj) and jj == 0):
                    pe.wait_ge(mask_copied, jj)
                for it in range(GI):
                    ins = nc.tensor.transpose(mT[:, it * P:(it + 1) * P],
                                              adj_b[:, c % NCB, it, (u % CJ) * P:(u % CJ + 1) * P], ident_b[:, :])
                ins.then_inc(mask_ready, 1)

            def clear_bank(pp, k):
                a, e = bank_pairs(k)
                w = (e - a) * 2 * AW
                if not (known(pp) and pp == 0):
                    if k in ACT_BANKS:
                        pe.wait_ge(acc_out_act, len(ACT_BANKS) * (pp - 1) + k + 1)
                    else:
                        pe.wait_ge(acc_out_dve, len(DVE_BANKS) * (pp - 1) + k - DVE_BANKS[0] + 1)
                nc.tensor.matmul(acc[k][:, 0:w], zeros[:, 0:P], zeros[:, 0:w], start=True, stop=True,
                                 skip_group_check=True)

            def products(b, g, p, u):
                uu = (b * NG + g) * UPG + p * NT + u
                if p == 0:
                    pe.wait_ge(mask_copied, (b * NG + g) * NT + u + 1)
                for it in range(GI):
                    for k in range(HP):
                        h = p * HP + k
                        if u == 0 and (it * HP + k) % PERBANK == 0:
                            clear_bank((b * NG + g) * NP + p, (it * HP + k) // PERBANK)
                        if apart(g, p) and k == 0:
                            continue
                        for part in range(2):
                            nc.tensor.matmul(acc_of(it, k, "F"), mask[:, u, it * P:(it + 1) * P],
                                             rf[:, u, h, part, :], start=False, stop=False, skip_group_check=True)
                pe.wait_ge(b_ready, uu + 1)
                if apart(g, p):
                    h = p * HP
                    for it in range(GI):
                        for part in range(2):
                            nc.tensor.matmul(acc_of(it, 0, "E"), b_pos[:, u % 2, 0, it * P:(it + 1) * P],
                                             rh[:, u, h, part, 0:AW], start=False, stop=False, skip_group_check=True)
                    pe.wait_ge(neg_ready, b * NT + u + 1)
                    for it in range(GI):
                        for part in range(2):
                            nc.tensor.matmul(acc_of(it, 0, "F"), b_neg[:, u % 2, it * P:(it + 1) * P],
                                             rf[:, u, h, part, :], start=False, stop=False, skip_group_check=True)
                for it in range(GI):
                    for k in range(HP):
                        h = p * HP + k
                        for part in range(2 if not (apart(g, p) and k == 0) else 0):
                            ins = nc.tensor.matmul(acc_of(it, k), b_pos[:, u % 2, k, it * P:(it + 1) * P],
                                                   rh[:, u, h, part, :], start=False, stop=False,
                                                   skip_group_check=True)
                        n = it * HP + k + 1
                        if u == NT - 1 and n % PERBANK == 0 and n < NPAIR:
                            ins.then_inc(bank_done, 1)
                ins.then_inc(pv_done, 1)

            transpose_x(0, 0)
            for q in range(HALF):
                if q + 1 < HALF:
                    transpose_x(0, q + 1)
                project(0, q, 0)
                project(0, q, 1)
            score_row(0)

            def body(b, first, last):
                for g in range(NG):
                    for p in range(NP):
                        pp = (b * NG + g) * NP + p
                        if g == 0:
                            pe.wait_ge(neg_done, b * NP + p + 1)
                        if first and g == 0 and p == 0:
                            transpose_mask(b, g, 0)
                            transpose_mask(b, g, 1)
                        for u in range(NT):
                            if not last and projection_step(g, p, u):
                                q, step = projection_step(g, p, u)
                                if step == 0:
                                    transpose_x(b + 1, q)
                                else:
                                    project(b + 1, q, step - 1)
                            if p == 0 and u + 2 < NT:
                                transpose_mask(b, g, u + 2)
                            if p == 1 and u >= NT - 2 and not (last and g == NG - 1):
                                transpose_mask(*((b, g + 1) if g + 1 < NG else (b + 1, 0)), u + 2 - NT)
                            products(b, g, p, u)
                            if g == 1 and p == 1 and not last and u == 3:
                                score_row(b + 1)

            batches(pe, body)

            pe.wait_ge(tested, 4)
            nc.tensor.matmul(pj[0:1, 0:1], beyond[:, :], ones[:, :], start=True, stop=True).then_inc(beyond_summed, 1)

            def general():
                with pe.Fori(0, B) as b:
                    with pe.Fori(0, NT) as t:
                        k = b * NT + t
                        pe.wait_ge(x_tile_loaded, 16 * (k + 1))
                        for c in range(DC):
                            ins = nc.tensor.transpose(pj[:, c * P:(c + 1) * P], x_pair[:, 0, c * P:(c + 1) * P],
                                                      ident_f[:, :])
                        ins.then_inc(x_tile_transposed, 1)
                        pe.wait_ge(x_tile_copied, k + 1)
                        for c in range(DC):
                            se = dict(start=(c == 0), stop=(c == DC - 1))
                            nc.tensor.matmul(pj[:, 0:HD], xT[:, 0, c, :], w_cat[:, c, 0:HD], **se)
                            nc.tensor.matmul(acc[0][:, 0:H * T], xT[:, 0, c, :], w_all[:, c, 0:H * T], **se)
                            ins = nc.tensor.matmul(acc[1][0:H * T, 0:P], w_all[:, c, H * T:ALLC], xT[:, 0, c, :], **se)
                        ins.then_inc(tile_products, 1)
                    with pe.Fori(0, H * NT) as n:
                        k = b * (H * NT) + n
                        pe.wait_ge(exp_done, k + 1)
                        for jt in range(NT):
                            ins = nc.tensor.transpose(acc[jt // 4][:, (jt % 4) * P:(jt % 4 + 1) * P],
                                                      g_w[:, jt * P:(jt + 1) * P], ident_f[:, :])
                        ins.then_inc(exp_transposed, 1)
                        pe.wait_ge(exp_copied, k + 1)
                        for jt in range(NT):
                            ins = nc.tensor.matmul(acc[4][:, 0:HO], g_expT[:, jt, :], g_head[:, jt, :],
                                                   start=(jt == 0), stop=(jt == NT - 1))
                        ins.then_inc(attention_product, 1)

            second_path(pe, general)


_INS = ['x', 'adj', 'L0_gnn_W', 'L0_gnn_a_src', 'L0_gnn_a_dst', 'L0_gnn_bias', 'L0_gnn_ln_gamma', 'L0_gnn_ln_beta']


def kernel(**inputs):
    import numpy as _np
    import concourse.bacc as _bacc
    from concourse import mybir as _mybir
    from concourse.bass_utils import run_bass_kernel_spmd as _run

    nc = _bacc.Bacc("TRN2", target_bir_lowering=False, num_devices=1)
    arrays, args = {}, []
    for name in _INS:
        a = _np.ascontiguousarray(inputs[name])
        arrays[f"in_{name}_dram"] = a
        args.append(nc.dram_tensor(f"in_{name}_dram", a.shape, _mybir.dt.from_np(a.dtype), kind="ExternalInput").ap())
    shape = inputs["x"].shape
    args.append(nc.dram_tensor("out_0_dram", shape, _mybir.dt.float32, kind="ExternalOutput").ap())
    nc.disable_value_cache = True
    gat_layer(nc, *args)
    r = _run(nc, [arrays], core_ids=[0])
    return r.results[0]["out_0_dram"]
```
